# Optimizing a Trainium2 kernel written in Bass

```python
import numpy as np
import jax
import jax.numpy as jnp

def _softmax(x, axis=-1):
    return jax.nn.softmax(x, axis=axis)

def _gelu(x):
    return jax.nn.gelu(x, approximate=True)

def _silu(x):
    return jax.nn.silu(x)

def _sigmoid(x):
    return jax.nn.sigmoid(x)

def _layernorm(x, axis=-1, eps=1e-05):
    m = jnp.mean(x, axis=axis, keepdims=True)
    v = jnp.var(x, axis=axis, keepdims=True)
    return (x - m) / jnp.sqrt(v + eps)

def _scatter_add(tgt, idx, src, axis=0):
    return tgt.at[idx].add(src)

def _segment_sum(src, seg, n):
    return jax.ops.segment_sum(src, seg, n)
kernel_name = 'mk_seq_preln_d1_jaxref_r4_521079'

def setup_inputs(seed: int=0):
    np.random.seed(seed)
    _w = jnp.asarray

    def _L0_attn_setup():
        import jax, jax.numpy as jnp
        import numpy as np
        import math
        HIDDEN = 256
        HEADS = 16
        HEAD_DIM = HIDDEN // HEADS
        MAX_POS = 512
        BATCH = 2
        SEQ = 512
        key = jax.random.key(seed)
        ks = jax.random.split(key, 8)
        s = 0.02
        return {'hidden_states': jax.random.normal(ks[0], (BATCH, SEQ, HIDDEN), jnp.float32), 'Wq': jax.random.normal(ks[1], (HIDDEN, HIDDEN), jnp.float32) * s, 'bq': jnp.zeros((HIDDEN,), jnp.float32), 'Wk': jax.random.normal(ks[2], (HIDDEN, HIDDEN), jnp.float32) * s, 'bk': jnp.zeros((HIDDEN,), jnp.float32), 'Wv': jax.random.normal(ks[3], (HIDDEN, HIDDEN), jnp.float32) * s, 'bv': jnp.zeros((HIDDEN,), jnp.float32), 'dist_emb': jax.random.normal(ks[4], (2 * MAX_POS - 1, HEAD_DIM), jnp.float32) * s}
    _L0_attn_in = _L0_attn_setup()

    def _L0_ffn_setup():
        import jax, jax.numpy as jnp
        import numpy as np
        TOP_K = 2
        key = jax.random.key(seed)
        ks = jax.random.split(key, 7)
        B, L, D, H, E, S = (2, 512, 256, 128, 16, 512)
        s = lambda fan_in: (1.0 / np.sqrt(fan_in)).astype(np.float32)
        return {'x': jax.random.normal(ks[0], (B, L, D), jnp.float32), 'gate_w': jax.random.normal(ks[1], (E, D), jnp.float32) * s(D), 'w1': jax.random.normal(ks[2], (E, H, D), jnp.float32) * s(D), 'w2': jax.random.normal(ks[3], (E, D, H), jnp.float32) * s(H), 'sfc1': jax.random.normal(ks[4], (S, D), jnp.float32) * s(D), 'sfc2': jax.random.normal(ks[5], (S, D), jnp.float32) * s(D), 'sfc3': jax.random.normal(ks[6], (D, S), jnp.float32) * s(S)}
    _L0_ffn_in = _L0_ffn_setup()
    _d = {'L0_attn_hidden_states': _L0_attn_in['hidden_states'], 'L0_attn_Wq': _L0_attn_in['Wq'], 'L0_attn_bq': _L0_attn_in['bq'], 'L0_attn_Wk': _L0_attn_in['Wk'], 'L0_attn_bk': _L0_attn_in['bk'], 'L0_attn_Wv': _L0_attn_in['Wv'], 'L0_attn_bv': _L0_attn_in['bv'], 'L0_attn_dist_emb': _L0_attn_in['dist_emb'], 'L0_ffn_gate_w': _L0_ffn_in['gate_w'], 'L0_ffn_w1': _L0_ffn_in['w1'], 'L0_ffn_w2': _L0_ffn_in['w2'], 'L0_ffn_sfc1': _L0_ffn_in['sfc1'], 'L0_ffn_sfc2': _L0_ffn_in['sfc2'], 'L0_ffn_sfc3': _L0_ffn_in['sfc3']}
    _x0 = _d['L0_attn_hidden_states']
    _d['L0_attn_hidden_states'] = jax.random.normal(jax.random.fold_in(jax.random.key(seed), 1), (8, 1024, 256), dtype=_x0.dtype)
    del _x0
    return _d

def reference(L0_attn_hidden_states, L0_attn_Wq, L0_attn_bq, L0_attn_Wk, L0_attn_bk, L0_attn_Wv, L0_attn_bv, L0_attn_dist_emb, L0_ffn_gate_w, L0_ffn_w1, L0_ffn_w2, L0_ffn_sfc1, L0_ffn_sfc2, L0_ffn_sfc3):

    def _L0_attn_ref(hidden_states, Wq, bq, Wk, bk, Wv, bv, dist_emb):
        import jax, jax.numpy as jnp
        import numpy as np
        import math
        HIDDEN = 256
        HEADS = 16
        HEAD_DIM = HIDDEN // HEADS
        MAX_POS = 512
        BATCH = 2
        SEQ = 512
        B, S, H = hidden_states.shape
        q = (hidden_states @ Wq.T + bq).reshape(B, S, HEADS, HEAD_DIM)
        k = (hidden_states @ Wk.T + bk).reshape(B, S, HEADS, HEAD_DIM)
        v = (hidden_states @ Wv.T + bv).reshape(B, S, HEADS, HEAD_DIM)
        scores = jnp.einsum('bqhd,bkhd->bhqk', q, k) / math.sqrt(HEAD_DIM)
        pos_q = jnp.arange(S)
        distance = pos_q[:, None] - pos_q[None, :]
        pos_emb = dist_emb[MAX_POS - 1 + distance]
        scores = scores + jnp.einsum('bqhd,qkd->bhqk', q, pos_emb)
        scores = scores + jnp.einsum('bkhd,qkd->bhqk', k, pos_emb)
        probs = jax.nn.softmax(scores, axis=-1)
        ctx = jnp.einsum('bhqk,bkhd->bqhd', probs, v)
        return ctx.reshape(B, S, H)

    def _L0_ffn_ref(x, gate_w, w1, w2, sfc1, sfc2, sfc3):
        import jax, jax.numpy as jnp
        import numpy as np
        TOP_K = 2
        B, L, D = x.shape
        E = gate_w.shape[0]
        shared = jnp.einsum('bls,ds->bld', jax.nn.silu(jnp.einsum('bld,sd->bls', x, sfc1)) * jnp.einsum('bld,sd->bls', x, sfc2), sfc3)
        logits = jnp.einsum('bld,ed->ble', x, gate_w)
        top_w, top_idx = jax.lax.top_k(logits, TOP_K)
        top_w = jax.nn.softmax(top_w, axis=-1)
        xf = x.reshape(-1, D)
        T = xf.shape[0]
        idx = top_idx.reshape(T, TOP_K)
        wk = top_w.reshape(T, TOP_K)
        dispatch = jnp.zeros((T, E), xf.dtype).at[jnp.arange(T)[:, None], idx].add(wk)
        h = jax.nn.silu(jnp.einsum('td,ehd->teh', xf, w1))
        moe = jnp.einsum('teh,te,edh->td', h, dispatch, w2)
        return moe.reshape(B, L, D) + shared
    x = L0_attn_hidden_states
    x = x + _L0_attn_ref(_layernorm(x, axis=-1), L0_attn_Wq, L0_attn_bq, L0_attn_Wk, L0_attn_bk, L0_attn_Wv, L0_attn_bv, L0_attn_dist_emb)
    x = x + _L0_ffn_ref(_layernorm(x, axis=-1), L0_ffn_gate_w, L0_ffn_w1, L0_ffn_w2, L0_ffn_sfc1, L0_ffn_sfc2, L0_ffn_sfc3)
    return x

_drawn_inputs = setup_inputs


def setup_inputs(seed=0):
    import zlib

    import numpy as np

    out = dict(_drawn_inputs(seed))
    spreads = {'L0_attn_bq': (0.0, 0.8), 'L0_attn_bk': (0.0, 0.8), 'L0_attn_bv': (0.0, 0.1)}
    factors = {'L0_attn_Wq': 3.877, 'L0_attn_Wk': 3.768, 'L0_attn_dist_emb': 8.0}
    for name, (base, spread) in spreads.items():
        noise = np.random.default_rng([zlib.crc32(name.encode()), seed]).standard_normal(out[name].shape)
        drawn = base * np.exp(spread * noise) if base else spread * noise
        out[name] = jnp.asarray(drawn.astype(out[name].dtype))
    for name, factor in factors.items():
        out[name] = (out[name] * factor).astype(out[name].dtype)
    return out
```

```python
from contextlib import ExitStack

import numpy as np

import concourse.bass as bass
from concourse import mybir
from concourse.alu_op_type import AluOpType as ALU

FP32 = mybir.dt.float32
BF16 = mybir.dt.bfloat16
U32 = mybir.dt.uint32
ACT = mybir.ActivationFunctionType
AXIS = mybir.AxisListType

P = 128
B, S, D = 8, 1024, 256
H, DH = 16, 16
BH = B * H
E, F = 16, 128
SH = 512
MAX_POS = 512
TABLE = 2 * S
EPS = 1e-5
DC = D // P
TOK = 512
TT = TOK // P
GROUPS = B * S // TOK
KT = S // P
PART_A = (0, 0, 1, 1, 0, 2)
PART_B = (0, 1, 0, 1, 2, 0)
ROWS = len(PART_A) * DH
HQ = 64
WIN = HQ + P - 1


def wait_count(engine, semaphore, count):
    if not (isinstance(count, int) and count <= 0):
        engine.wait_ge(semaphore, count)


def wait_apart(engine, semaphore, count, passed):
    wait_count(engine, semaphore, count)
    if not isinstance(count, int):
        engine.sem_inc(passed, 1)


def _bank_pair(ctx, nc, name):
    return ctx.enter_context(nc.psum_tensor(name, [P, 2, 512], FP32))


def project(nc, io, scratch):
    with ExitStack() as ctx:
        def sb(name, shape, dt=FP32):
            return ctx.enter_context(nc.sbuf_tensor(name, shape, dt))

        def sem(name):
            return ctx.enter_context(nc.semaphore(name))

        ident = sb("p_ident", [P, P])
        wq, wk, wv = (sb(n, [P, DC, D]) for n in ("wq_sb", "wk_sb", "wv_sb"))
        bias_q, bias_k, bias_k4 = (sb(n, [P, DC]) for n in ("bias_q", "bias_k", "bias_k4"))
        bias_v = sb("bias_v", [P, D])
        minus_half = sb("p_minus_half", [P, TT])
        x_sb = sb("p_x", [P, 2, TT, D])
        xn = sb("p_xn", [P, 2, TT, D])
        stats = sb("p_stats", [P, 2, TT, 6])
        moments = sb("p_moments", [P, 2, TT, 2])
        var_eps = sb("p_var_eps", [P, 2, TT])
        rstd = sb("p_rstd", [P, 2, TT])
        xT = sb("p_xT", [P, 2, DC, TOK])
        qk32 = sb("qk32", [P, 4 * TOK])
        rest = sb("rest", [P, 4 * TOK])
        parts = sb("parts", [P, 2, 3, 4, TOK], BF16)
        v_sb = sb("p_v", [P, 2, TT, D])
        table = sb("table", [DH, 2, TABLE])
        table_parts = sb("table_parts", [DH, 3, 2, TABLE], BF16)

        psT = ctx.enter_context(nc.psum_tensor("p_psT", [P, DC, TOK], FP32))
        psQK = ctx.enter_context(nc.psum_tensor("psQK", [P, 4, TOK], FP32))
        psV = ctx.enter_context(nc.psum_tensor("psV", [P, TT, D], FP32))

        weights_in, table_in, tables_out = sem("weights_in"), sem("table_in"), sem("tables_out")
        x_in = [sem("x_in0"), sem("x_in1")]
        consts_set, table_step, part_cut, bias_set = sem("consts_set"), sem("table_step"), sem("part_cut"), sem("bias_set")
        stat_step, var_ready, rstd_ready, xn_ready = sem("stat_step"), sem("var_ready"), sem("rstd_ready"), sem("xn_ready")
        xT_psum, xT_ready, qk_psum, v_psum = sem("xT_psum"), sem("xT_ready"), sem("qk_psum"), sem("v_psum")
        qk32_ready, part1, rest1, part2, rest2, part3 = (
            sem(n) for n in ("qk32_ready", "part1", "rest1", "part2", "rest2", "part3"))
        v_ready = sem("v_ready")
        dve_passed, pool_passed = sem("p_dve_passed"), sem("p_pool_passed")
        stored = [sem("stored0"), sem("stored1")]
        STORES = 3 * len(PART_A) + 1

        with nc.Block() as block:
            @block.sync
            def _(sp):
                sp.dma_start(ident[:, :], io["ident"]).then_inc(weights_in, 16)
                for w, name in ((wq, "wq_t"), (wk, "wk_t"), (wv, "wv_t")):
                    sp.dma_start(w[:, :, :], io[name].rearrange("(c p) n -> p c n", p=P)).then_inc(weights_in, 16)
                for bias, name in ((bias_q, "bq"), (bias_k, "bk")):
                    with nc.allow_non_contiguous_dma(reason="256 biases, once"):
                        sp.dma_start(bias[:, :], io[name].rearrange("(c p) -> p c", p=P)).then_inc(weights_in, 16)
                sp.dma_start(bias_v[:, :], io["bv"].rearrange("(a n) -> a n", a=1).to_broadcast([P, D])).then_inc(weights_in, 16)
                low = S - MAX_POS
                n = 2 * MAX_POS - 1
                sp.dma_start(table[:, 1, 0:low], io["dist_t"][:, n - low:n]).then_inc(table_in, 16)
                sp.dma_start(table[:, 1, low:low + n], io["dist_t"]).then_inc(table_in, 16)
                sp.dma_start(table[:, 0, S - MAX_POS:S - MAX_POS + n], io["dist_rev"]).then_inc(table_in, 16)
                sp.dma_start(table[:, 0, S - MAX_POS + n:S - MAX_POS + n + low], io["dist_rev"][:, 0:low]).then_inc(table_in, 16)
                sp.wait_ge(part_cut, 3)
                for g, part in enumerate(PART_B):
                    for way in range(2):
                        sp.dma_start(scratch["tables"][way, g * DH:(g + 1) * DH, :],
                                     table_parts[:, part, way, :]).then_inc(tables_out, 16)

                def load_x(b, par):
                    sp.dma_start(x_sb[:, par], io["x"][bass.ds(b, 1), par * TOK:(par + 1) * TOK, :].rearrange(
                        "o (t p) d -> p (o t) d", p=P)).then_inc(x_in[par], 16)

                def store(b, par):
                    g = b * 2 + par
                    sp.wait_ge(v_ready, g + 1)
                    sp.dma_start(scratch["v"][bass.ds(b, 1), :, par * TT:(par + 1) * TT, :].rearrange("o p t n -> p (o t) n"),
                                 v_sb[:, par]).then_inc(stored[par], 16)
                    sp.wait_ge(part2, g + 1)
                    sp.wait_ge(part3, g + 1)
                    for rows, pattern, first in (("q_a", PART_A, 0), ("k_a", PART_A, 2), ("k_b", PART_B, 2)):
                        for i, part in enumerate(pattern):
                            dst = scratch[rows][i, bass.ds(b * H, H), :, par * TOK:(par + 1) * TOK]
                            sp.dma_start(dst.rearrange("(half h) d s -> (h d) half s", half=2),
                                         parts[:, par, part, first:first + 2, :]).then_inc(stored[par], 16)

                load_x(0, 0)
                load_x(0, 1)
                with sp.Fori(0, B - 1) as b:
                    for par in range(2):
                        sp.wait_ge(xn_ready, b * 2 + par + 1)
                        load_x(b + 1, par)
                        store(b, par)
                for par in range(2):
                    store(B - 1, par)
                for par in range(2):
                    sp.wait_ge(stored[par], B * STORES * 16)
                sp.wait_ge(tables_out, 16 * 2 * len(PART_B))

            @block.gpsimd
            def _(pool):
                nc.gpsimd.memset(minus_half[:, :], -0.5).then_inc(consts_set, 1)
                pool.wait_ge(consts_set, 1)
                with pool.Fori(0, B) as b:
                    for par in range(2):
                        g = b * 2 + par
                        pool.wait_ge(var_ready, g + 1)
                        nc.gpsimd.tensor_tensor(rstd[:, par], var_eps[:, par], minus_half[:, :], ALU.pow).then_inc(rstd_ready, 1)
                        wait_apart(pool, rest1, g + 1, pool_passed)
                        nc.gpsimd.tensor_copy(parts[:, par, 1].rearrange("p a t -> p (a t)"), rest[:, :]).then_inc(part2, 1)
                        wait_apart(pool, rest2, g + 1, pool_passed)
                        nc.gpsimd.tensor_copy(parts[:, par, 2].rearrange("p a t -> p (a t)"), rest[:, :]).then_inc(part3, 1)

            @block.vector
            def _(dve):
                dve.wait_ge(table_in, 64)
                n = 2 * MAX_POS - 1
                end = S - MAX_POS + n
                nc.vector.tensor_copy(table[:, 1, end:TABLE], table[:, 1, end - 1:end].to_broadcast([DH, TABLE - end])).then_inc(table_step, 1)
                first = S - MAX_POS
                nc.vector.tensor_copy(table[:, 0, 0:first], table[:, 0, first:first + 1].to_broadcast([DH, first])).then_inc(table_step, 1)
                nc.vector.memset(table[:, 0, TABLE - 1:TABLE], 0.0).then_inc(table_step, 1)
                dve.wait_ge(table_step, 3)
                nc.vector.tensor_scalar(table[:, 0, :], table[:, 0, :], -1.0, None, ALU.mult).then_inc(table_step, 1)
                nc.vector.tensor_scalar(table[:, 1, :], table[:, 1, :], 4.0, None, ALU.mult).then_inc(table_step, 1)
                for part in range(3):
                    dve.wait_ge(table_step, 5 + part)
                    ins = nc.vector.tensor_copy(table_parts[:, part], table[:, :, :])
                    ins.then_inc(part_cut, 1)
                    if part < 2:
                        dve.wait_ge(part_cut, part + 1)
                        nc.vector.tensor_tensor(table[:, :, :], table[:, :, :], table_parts[:, part], ALU.subtract).then_inc(table_step, 1)
                dve.wait_ge(weights_in, 7 * 16)
                nc.vector.tensor_scalar(bias_k4[:, :], bias_k[:, :], -0.25, None, ALU.mult).then_inc(bias_set, 1)
                with dve.Fori(0, B) as b:
                    for par in range(2):
                        g = b * 2 + par
                        dve.wait_ge(x_in[par], b * 16 + 16)
                        for t in range(TT):
                            nc.vector.bn_stats(stats[:, par, t], x_sb[:, par, t]).then_inc(stat_step, 1)
                        for t in range(TT):
                            wait_apart(dve, stat_step, g * 2 * TT + t + 1, dve_passed)
                            nc.vector.bn_aggr(moments[:, par, t], stats[:, par, t]).then_inc(stat_step, 1)
                        dve.wait_ge(stat_step, g * 2 * TT + 2 * TT)
                        nc.vector.tensor_scalar(var_eps[:, par], moments[:, par, :, 1], EPS, None, ALU.add).then_inc(var_ready, 1)
                        dve.wait_ge(rstd_ready, g + 1)
                        for t in range(TT):
                            ins = nc.vector.tensor_scalar(xn[:, par, t], x_sb[:, par, t], moments[:, par, t, 0:1],
                                                          rstd[:, par, t:t + 1], ALU.subtract, ALU.mult)
                        ins.then_inc(xn_ready, 1)
                        dve.wait_ge(part1, g + 1)
                        dve.wait_ge(part3, g)
                        nc.vector.tensor_tensor(rest[:, :], qk32[:, :], parts[:, par, 0].rearrange("p a t -> p (a t)"),
                                                ALU.subtract).then_inc(rest1, 1)
                        dve.wait_ge(v_psum, g + 1)
                        dve.wait_ge(stored[par], b * STORES * 16)
                        nc.vector.tensor_tensor(v_sb[:, par], psV[:, :, :], bias_v[:, None, :].to_broadcast([P, TT, D]),
                                                ALU.add).then_inc(v_ready, 1)
                        dve.wait_ge(part2, g + 1)
                        nc.vector.tensor_tensor(rest[:, :], rest[:, :], parts[:, par, 1].rearrange("p a t -> p (a t)"),
                                                ALU.subtract).then_inc(rest2, 1)

            @block.tensor
            def _(pe):
                pe.wait_ge(weights_in, 7 * 16)
                with pe.Fori(0, B) as b:
                    for par in range(2):
                        g = b * 2 + par
                        pe.wait_ge(xn_ready, g + 1)
                        for c in range(DC):
                            for t in range(TT):
                                ins = nc.tensor.transpose(psT[:, c, t * P:(t + 1) * P], xn[:, par, t, c * P:(c + 1) * P], ident[:, :])
                        ins.then_inc(xT_psum, 1)
                        pe.wait_ge(xT_ready, g + 1)
                        pe.wait_ge(qk32_ready, g * 4)
                        for slot in range(4):
                            w, half = (wq, wk)[slot // 2], slot % 2
                            for c in range(DC):
                                ins = nc.tensor.matmul(psQK[:, slot, :], w[:, c, half * P:(half + 1) * P], xT[:, par, c, :],
                                                       start=c == 0, stop=c == DC - 1)
                            ins.then_inc(qk_psum, 1)
                        pe.wait_ge(v_ready, g)
                        for t in range(TT):
                            for c in range(DC):
                                ins = nc.tensor.matmul(psV[:, t, :], xT[:, par, c, t * P:(t + 1) * P], wv[:, c, :],
                                                       start=c == 0, stop=c == DC - 1)
                        ins.then_inc(v_psum, 1)

            @block.scalar
            def _(act):
                act.wait_ge(weights_in, 7 * 16)
                act.wait_ge(bias_set, 1)
                with act.Fori(0, B) as b:
                    for par in range(2):
                        g = b * 2 + par
                        act.wait_ge(xT_psum, g + 1)
                        nc.scalar.activation(xT[:, par], psT[:, :, :], ACT.Copy).then_inc(xT_ready, 1)
                        act.wait_ge(rest1, g)
                        for slot in range(4):
                            bias, scale = ((bias_q, 1.0), (bias_k4, -0.25))[slot // 2]
                            act.wait_ge(qk_psum, g * 4 + slot + 1)
                            nc.scalar.activation(qk32[:, slot * TOK:(slot + 1) * TOK], psQK[:, slot, :], ACT.Identity,
                                                 bias=bias[:, slot % 2:slot % 2 + 1], scale=scale).then_inc(qk32_ready, 1)
                        act.wait_ge(qk32_ready, g * 4 + 4)
                        act.wait_ge(stored[par], b * STORES * 16)
                        nc.scalar.activation(parts[:, par, 0].rearrange("p a t -> p (a t)"), qk32[:, :], ACT.Copy).then_inc(part1, 1)


def reblock_queries(nc, scratch):
    with nc.semaphore("blocks_out") as blocks_out, nc.Block() as block:
        @block.sync
        def _(sp):
            with sp.Fori(0, S // HQ) as q:
                for g in range(len(PART_A)):
                    sp.dma_start(scratch["q_blocks"][bass.ds(q, 1), g * DH:(g + 1) * DH].rearrange("o d h s -> (o d) h s"),
                                 scratch["q_a"][g, :, :, bass.ds(q * HQ, HQ)].rearrange("h d s -> d h s")).then_inc(blocks_out, 16)
            sp.wait_ge(blocks_out, 16 * len(PART_A) * (S // HQ))


def position(nc, scratch):
    HALVES = 2
    STEPS = 8
    QS, KS = HQ // STEPS, P // STEPS
    with ExitStack() as ctx:
        def sb(name, shape, dt=FP32):
            return ctx.enter_context(nc.sbuf_tensor(name, shape, dt))

        def sem(name):
            return ctx.enter_context(nc.semaphore(name))

        queries = [sb(f"queries{h}", [ROWS, BH, HQ], BF16) for h in range(HALVES)]
        keys = sb("keys", [ROWS, BH, P], BF16)
        falling = [sb(f"falling{h}", [ROWS, WIN], BF16) for h in range(HALVES)]
        rising = [sb(f"rising{h}", [ROWS, WIN], BF16) for h in range(HALVES)]
        z = [sb(f"z{h}", [P, HQ, P]) for h in range(HALVES)]
        q_ps = [_bank_pair(ctx, nc, f"q_ps{i}") for i in range(2)]
        k_ps = [_bank_pair(ctx, nc, f"k_ps{i}") for i in range(2)]

        keys_in = sem("keys_in")
        queries_in = [sem(f"queries_in{h}") for h in range(HALVES)]
        rising_in = [sem(f"rising_in{h}") for h in range(HALVES)]
        z_out = [sem(f"z_out{h}") for h in range(HALVES)]
        pe_passed, sp_passed = sem("z_pe_passed"), sem("z_sp_passed")
        q_terms, q_copied, k_terms, k_added = sem("q_terms"), sem("q_copied"), sem("k_terms"), sem("k_added")

        with nc.Block() as block:
            @block.sync
            def _(sp):
                def load_queries(kt, qt, half):
                    sp.dma_start(queries[half][:, :, :],
                                 scratch["q_blocks"][bass.ds(qt * HALVES + half, 1)].rearrange("o r h s -> (o r) h s")
                                 ).then_inc(queries_in[half], 16)
                    sp.dma_start(falling[half][:, :],
                                 scratch["tables"][0, :, bass.ds(S - HQ - half * HQ + (kt - qt) * P, WIN)]
                                 ).then_inc(queries_in[half], 16)

                def load_rising(kt, qt, half):
                    sp.dma_start(rising[half][:, :],
                                 scratch["tables"][1, :, bass.ds(S - P + half * HQ + (qt - kt) * P, WIN)]
                                 ).then_inc(rising_in[half], 16)

                for half in range(HALVES):
                    load_queries(0, 0, half)
                    load_rising(0, 0, half)
                with sp.Fori(0, KT) as kt:
                    wait_apart(sp, k_terms, kt * (KT * HALVES * STEPS), sp_passed)
                    for g in range(len(PART_A)):
                        sp.dma_start(keys[g * DH:(g + 1) * DH, :, :],
                                     scratch["k_a"][g, :, :, bass.ds(kt * P, P)].rearrange("h d s -> d h s")).then_inc(keys_in, 16)
                    for zpart in range(2):
                        with sp.Fori(0, KT // 2) as row:
                            qt = row + zpart * (KT // 2)
                            n = kt * KT + qt
                            nxt = (n + 1) % (KT * KT)
                            for half in range(HALVES):
                                wait_apart(sp, q_terms, (n * HALVES + half + 1) * STEPS, sp_passed)
                                load_queries(nxt // KT, nxt % KT, half)
                                sp.wait_ge(k_added, (n * HALVES + half + 1) * STEPS)
                                sp.dma_start(scratch["z"][zpart][:, bass.ds(row * P + half * HQ, HQ), bass.ds(kt * P, P)],
                                             z[half][:, :, :]).then_inc(z_out[half], 16)
                                load_rising(nxt // KT, nxt % KT, half)
                for half in range(HALVES):
                    sp.wait_ge(z_out[half], KT * KT * 16)
                    sp.wait_ge(queries_in[half], (KT * KT + 1) * 32)
                    sp.wait_ge(rising_in[half], (KT * KT + 1) * 16)

            @block.tensor
            def _(pe):
                def query_terms(m, half, step):
                    slot = step % 2
                    if isinstance(m, int):
                        if step >= 2:
                            pe.wait_ge(q_copied, step - 1)
                    else:
                        pe.wait_ge(q_copied, m * STEPS + step - 1)
                    for i in range(QS):
                        q = step * QS + i
                        ins = nc.tensor.matmul(q_ps[slot][:, i // 4, (i % 4) * P:(i % 4 + 1) * P], queries[half][:, :, q],
                                               falling[half][:, HQ - 1 - q:HQ - 1 - q + P], start=True, stop=True)
                    ins.then_inc(q_terms, 1)

                def key_terms(m, half, step):
                    slot = step % 2
                    pe.wait_ge(k_added, m * STEPS + max(step - 1, 0))
                    for i in range(KS):
                        k = step * KS + i
                        ins = nc.tensor.matmul(k_ps[slot][:, i // 8, (i % 8) * HQ:(i % 8 + 1) * HQ], keys[:, :, k],
                                               rising[half][:, P - 1 - k:P - 1 - k + HQ], start=True, stop=True)
                    ins.then_inc(k_terms, 1)

                pe.wait_ge(queries_in[0], 32)
                for step in range(STEPS):
                    query_terms(0, 0, step)
                with pe.Fori(0, KT) as kt:
                    wait_apart(pe, keys_in, (kt + 1) * len(PART_A) * 16, pe_passed)
                    with pe.Fori(0, KT) as qt:
                        n = kt * KT + qt
                        for half in range(HALVES):
                            pe.wait_ge(rising_in[half], (n + 1) * 16)
                            pe.wait_ge(queries_in[1 - half], (n + 1 + half) * 32)
                            for step in range(STEPS):
                                query_terms(n * HALVES + half + 1, 1 - half, step)
                                key_terms(n * HALVES + half, half, step)

            @block.scalar
            def _(act):
                def copy(m, half, step):
                    act.wait_ge(q_terms, m * STEPS + step + 1)
                    nc.scalar.activation(z[half][:, step * QS:(step + 1) * QS, :],
                                         q_ps[step % 2][:, :, :].rearrange("p a (q k) -> p (a q) k", k=P), ACT.Copy).then_inc(q_copied, 1)

                for step in range(STEPS):
                    copy(0, 0, step)
                with act.Fori(0, KT * KT) as n:
                    for half in range(HALVES):
                        act.wait_ge(z_out[1 - half], (n + half) * 16)
                        for step in range(STEPS):
                            copy(n * HALVES + half + 1, 1 - half, step)

            @block.vector
            def _(dve):
                with dve.Fori(0, KT * KT) as n:
                    for half in range(HALVES):
                        m = n * HALVES + half
                        dve.wait_ge(q_copied, (m + 1) * STEPS)
                        for step in range(STEPS):
                            dve.wait_ge(k_terms, m * STEPS + step + 1)
                            part = z[half][:, :, step * KS:(step + 1) * KS].rearrange("p q k -> p k q")
                            nc.vector.tensor_tensor(part, k_ps[step % 2][:, :, :].rearrange("p a (k q) -> p (a k) q", q=HQ),
                                                    part, ALU.add).then_inc(k_added, 1)


def attend(nc, io, scratch, ctx_all):
    GT = 4
    VW = 32
    HALF = KT // 2
    ZSLOTS = 4
    with ExitStack() as ctx:
        def sb(name, shape, dt=FP32):
            return ctx.enter_context(nc.sbuf_tensor(name, shape, dt))

        def sem(name):
            return ctx.enter_context(nc.semaphore(name))

        ident = sb("a_ident", [P, P])
        q_rows = [sb(f"q_rows{i}", [ROWS, S], BF16) for i in range(2)]
        k_rows = [sb(f"k_rows{i}", [ROWS, S], BF16) for i in range(2)]
        z = [sb(f"a_z{i}", [P, S]) for i in range(ZSLOTS)]
        scores = [sb(f"scores{i}", [P, S]) for i in range(2)]
        minus_max = sb("minus_max", [P, GT])
        probs = [sb(f"probs{i}", [P, S]) for i in range(2)]
        probs_t = [sb(f"probs_t{i}", [P, KT, GT * P]) for i in range(2)]
        v_batch = sb("v_batch", [P, 2, KT, H, DH])
        v_head = [sb(f"v_head{i}", [P, KT, VW]) for i in range(2)]
        pv_sb = sb("pv_sb", [P, P])
        inv_sum = sb("inv_sum", [P, GT])

        qk_ps = [_bank_pair(ctx, nc, f"qk_ps{i}") for i in range(2)]
        pt_ps = [ctx.enter_context(nc.psum_tensor(f"pt_ps{i}", [P, HALF, P], FP32)) for i in range(2)]
        pv_ps = ctx.enter_context(nc.psum_tensor("pv_ps", [P, 512], FP32))
        back_ps = ctx.enter_context(nc.psum_tensor("back_ps", [P, 512], FP32))

        ident_in, v_in, v_head_ready, v_head_set = sem("ident_in"), sem("v_in"), sem("v_head_ready"), sem("v_head_set")
        rows_in = [sem(f"rows_in{i}") for i in range(2)]
        z_in = [sem(f"z_in{i}") for i in range(ZSLOTS)]
        dve_passed, pool_passed = sem("a_dve_passed"), sem("a_pool_passed")
        qk_done, scores_ready, exp_done = sem("qk_done"), sem("scores_ready"), sem("exp_done")
        transposed = [sem(f"transposed{i}") for i in range(2)]
        copied = [sem(f"copied{i}") for i in range(2)]
        pv_done, pv_copied, back_done, inv_ready, ctx_written = (
            sem(n) for n in ("pv_done", "pv_copied", "back_done", "inv_ready", "ctx_written"))

        with nc.Block() as block:
            @block.sync
            def _(sp):
                def load_rows(h, slot):
                    for rows, name in ((q_rows, "q_a"), (k_rows, "k_b")):
                        sp.dma_start(rows[slot][:, :], scratch[name][:, bass.ds(h, 1)].rearrange("g o d s -> (g o) d s")
                                     ).then_inc(rows_in[slot], 16)

                def load_z(h, t):
                    sp.dma_start(z[t % ZSLOTS][:, :], scratch["z"][t // HALF][bass.ds(h, 1), (t % HALF) * P:(t % HALF + 1) * P, :].rearrange(
                        "o q k -> (o q) k")).then_inc(z_in[t % ZSLOTS], 16)

                def head(h, slot, last=False):
                    if not last:
                        wait_count(sp, qk_done, h * KT)
                        load_rows(h + 1, 1 - slot)
                    for t in range(KT):
                        if not (last and t >= KT - ZSLOTS):
                            sp.wait_ge(scores_ready, h * KT + t + 1)
                            load_z(h + (t + ZSLOTS) // KT, (t + ZSLOTS) % KT)

                sp.dma_start(ident[:, :], io["ident"]).then_inc(ident_in, 16)
                load_rows(0, 0)
                for t in range(ZSLOTS):
                    load_z(0, t)
                head(0, 0)
                with sp.Fori(0, BH // 2 - 1) as i:
                    head(i * 2 + 1, 1)
                    head(i * 2 + 2, 0)
                head(BH - 1, 1, last=True)

            @block.gpsimd
            def _(pool):
                def load_v(b):
                    pool.dma_start(v_batch[:, bass.ds(b % 2, 1)].rearrange("p o t h d -> p (o t) (h d)"),
                                   scratch["v"][bass.ds(b % B, 1)].rearrange("o p t n -> (o p) t n")).then_inc(v_in, 16)

                def head_v(b, h):
                    for slot in range(2):
                        n = b * H + h
                        wait_apart(pool, pv_done, n * 2 - 1 + slot, pool_passed)
                        nc.gpsimd.tensor_copy(v_head[slot][:, :, 0:DH],
                                              v_batch[:, bass.ds(b % 2, 1), :, bass.ds(h, 1), :].rearrange("p o t i d -> p (o t i) d")
                                              ).then_inc(v_head_ready, 1)

                for slot in range(2):
                    nc.gpsimd.memset(v_head[slot][:, :, :], 0.0).then_inc(v_head_set, 1)
                pool.wait_ge(v_head_set, 2)
                for slot in range(2):
                    nc.gpsimd.memset(v_head[slot][:, :, DH:DH + 1], 1.0).then_inc(v_head_set, 1)
                pool.wait_ge(v_head_set, 4)
                load_v(0)
                pool.wait_ge(v_in, 16)
                head_v(0, 0)
                with pool.Fori(1, H) as h:
                    head_v(0, h)
                with pool.Fori(1, B) as b:
                    load_v(b)
                    wait_apart(pool, v_in, b * 16 + 16, pool_passed)
                    with pool.Fori(0, H) as h:
                        head_v(b, h)

            @block.tensor
            def _(pe):
                def scores_of(h, t, slot):
                    n = h * KT + t
                    if t == 0:
                        pe.wait_ge(rows_in[slot], (h // 2 + 1) * 32)
                    wait_count(pe, scores_ready, n - 1)
                    for c in range(S // 512):
                        ins = nc.tensor.matmul(qk_ps[t % 2][:, c, :], q_rows[slot][:, t * P:(t + 1) * P],
                                               k_rows[slot][:, c * 512:(c + 1) * 512], start=True, stop=True)
                    ins.then_inc(qk_done, 1)

                def transpose_probs(h, t):
                    n = h * KT + t
                    pe.wait_ge(exp_done, n + 1)
                    for half in range(2):
                        wait_count(pe, copied[half], n)
                        for k in range(HALF):
                            kt = half * HALF + k
                            ins = nc.tensor.transpose(pt_ps[half][:, k, :], probs[t % 2][:, kt * P:(kt + 1) * P], ident[:, :])
                        ins.then_inc(transposed[half], 1)

                def products(g, slot, part):
                    if part == 0:
                        for half in range(2):
                            pe.wait_ge(copied[half], (g + 1) * GT)
                        pe.wait_ge(v_head_ready, g + 1)
                        wait_count(pe, pv_copied, g)
                    for kt in range(part * 2, part * 2 + 2):
                        for j in range(GT):
                            ins = nc.tensor.matmul(pv_ps[j * VW:(j + 1) * VW, 0:P], v_head[slot][:, kt, :],
                                                   probs_t[slot][:, kt, j * P:(j + 1) * P], start=kt == 0, stop=kt == KT - 1)
                    if part == GT - 1:
                        ins.then_inc(pv_done, 1)

                def transpose_back(g):
                    pe.wait_ge(pv_copied, g + 1)
                    wait_count(pe, ctx_written, g)
                    nc.tensor.transpose(back_ps[:, 0:P], pv_sb[:, :], ident[:, :]).then_inc(back_done, 1)

                def head(h, slot, first=False, last=False):
                    for t in range(KT):
                        g = h * 2 + t // GT
                        if t < KT - 1:
                            scores_of(h, t + 1, slot)
                        elif not last:
                            scores_of(h + 1, 0, 1 - slot)
                        transpose_probs(h, t)
                        if not (first and t < GT):
                            products(g - 1, 1 - t // GT, t % GT)
                        if not first and t % GT == 1:
                            transpose_back(g - 2)

                pe.wait_ge(ident_in, 16)
                scores_of(0, 0, 0)
                head(0, 0, first=True)
                with pe.Fori(0, BH // 2 - 1) as i:
                    head(i * 2 + 1, 1)
                    head(i * 2 + 2, 0)
                head(BH - 1, 1, last=True)
                groups = BH * 2
                transpose_back(groups - 2)
                for part in range(GT):
                    products(groups - 1, 1, part)
                transpose_back(groups - 1)

            @block.scalar
            def _(act):
                def exponentials(h, t):
                    n = h * KT + t
                    act.wait_ge(scores_ready, n + 1)
                    wait_count(act, transposed[1], n - 1)
                    nc.scalar.activation(probs[t % 2][:, :], scores[t % 2][:, :], ACT.Exp, scale=-1.0,
                                         bias=minus_max[:, t % GT:t % GT + 1]).then_inc(exp_done, 1)

                def copy_half(h, t):
                    n, g = h * KT + t, h * 2 + t // GT
                    act.wait_ge(transposed[0], n + 1)
                    if t % GT == 0:
                        wait_count(act, pv_done, g - 1)
                    nc.scalar.activation(probs_t[t // GT][:, 0:HALF, (t % GT) * P:(t % GT + 1) * P], pt_ps[0][:, :, :],
                                         ACT.Copy).then_inc(copied[0], 1)

                def copy_products(g):
                    act.wait_ge(pv_done, g + 1)
                    wait_count(act, back_done, g)
                    nc.scalar.activation(pv_sb[:, :], pv_ps[:, 0:P], ACT.Copy).then_inc(pv_copied, 1)

                def head(h, first=False):
                    for t in range(KT):
                        exponentials(h, t)
                        if t % GT == 0 and not first:
                            copy_products(h * 2 + t // GT - 2)
                        if t > 0:
                            copy_half(h, t - 1)
                        elif not first:
                            copy_half(h - 1, KT - 1)

                head(0, first=True)
                with act.Fori(0, BH // 2 - 1) as i:
                    head(i * 2 + 1)
                    head(i * 2 + 2)
                head(BH - 1)
                groups = BH * 2
                copy_products(groups - 2)
                copy_half(BH - 1, KT - 1)
                copy_products(groups - 1)

            @block.vector
            def _(dve):
                def add_positions(h, t):
                    n = h * KT + t
                    dve.wait_ge(z_in[t % ZSLOTS], (h * 2 + t // ZSLOTS + 1) * 16)
                    dve.wait_ge(qk_done, n + 1)
                    wait_apart(dve, exp_done, n - 1, dve_passed)
                    nc.vector.tensor_tensor_reduce(
                        out=scores[t % 2][:, :], in0=qk_ps[t % 2][:, :, :].rearrange("p a k -> p (a k)"), in1=z[t % ZSLOTS][:, :],
                        scale=1.0, scalar=3.0e38, op0=ALU.add, op1=ALU.min,
                        accum_out=minus_max[:, t % GT:t % GT + 1]).then_inc(scores_ready, 1)

                def copy_half(h, t):
                    n, g = h * KT + t, h * 2 + t // GT
                    dve.wait_ge(transposed[1], n + 1)
                    if t % GT == 0:
                        wait_count(dve, pv_done, g - 1)
                    nc.vector.tensor_copy(probs_t[t // GT][:, HALF:KT, (t % GT) * P:(t % GT + 1) * P], pt_ps[1][:, :, :]
                                          ).then_inc(copied[1], 1)

                def normalise(h, g, half):
                    dve.wait_ge(back_done, g + 1)
                    back = back_ps[:, 0:P].rearrange("q (j v) -> q j v", v=VW)
                    nc.vector.reciprocal(inv_sum[:, :], back[:, :, DH]).then_inc(inv_ready, 1)
                    dve.wait_ge(inv_ready, g + 1)
                    out = ctx_all[:, bass.ds(h, 1), half * GT:(half + 1) * GT, :].rearrange("p o j d -> p (o j) d")
                    nc.vector.tensor_tensor(out, back[:, :, 0:DH], inv_sum[:, :, None].to_broadcast([P, GT, DH]), ALU.mult
                                            ).then_inc(ctx_written, 1)

                def head(h, first=False):
                    for t in range(KT):
                        add_positions(h, t)
                        if t > 0:
                            copy_half(h, t - 1)
                        elif not first:
                            copy_half(h - 1, KT - 1)
                        if t % GT == 2 and not first:
                            normalise(h - 1, h * 2 + t // GT - 2, t // GT)

                head(0, first=True)
                with dve.Fori(0, BH // 2 - 1) as i:
                    head(i * 2 + 1)
                    head(i * 2 + 2)
                head(BH - 1)
                groups = BH * 2
                copy_half(BH - 1, KT - 1)
                normalise(BH - 1, groups - 2, 0)
                normalise(BH - 1, groups - 1, 1)


def mix(nc, io, ctx_all):
    SU = SH // P
    UNITS = SU + E
    with ExitStack() as ctx:
        def sb(name, shape, dt=FP32):
            return ctx.enter_context(nc.sbuf_tensor(name, shape, dt))

        def sem(name):
            return ctx.enter_context(nc.semaphore(name))

        ident = sb("m_ident", [P, P])
        ident16 = sb("m_ident16", [P, P], BF16)
        select = sb("select", [3 * E, E, P], BF16)
        iota = sb("iota", [P, TT, E])
        minus_half = sb("m_minus_half", [P, TT])
        gate = sb("gate", [P, DC, E])
        w1 = sb("w1_sb", [P, DC, E, F])
        w2 = sb("w2_sb", [P, E, D])
        sfc1, sfc2 = (sb(n, [P, DC, SH]) for n in ("sfc1_sb", "sfc2_sb"))
        sfc3 = sb("sfc3_sb", [P, SU, D])
        x_sb = sb("m_x", [P, 2, TT, D])
        x2 = sb("x2", [P, 2, TT, D])
        xn = sb("m_xn", [P, TT, D])
        stats = sb("m_stats", [P, TT, 6])
        moments = sb("m_moments", [P, TT, 2])
        var_eps = sb("m_var_eps", [P, TT])
        rstd = sb("m_rstd", [P, TT])
        xT = sb("m_xT", [P, DC, TOK])
        logits = sb("logits", [P, TT, E])
        top = sb("top", [P, TT, 8])
        top_at = sb("top_at", [P, TT, 8], U32)
        top_atf = sb("top_atf", [P, TT, 2])
        gap = sb("gap", [P, TT])
        gap_exp = sb("gap_exp", [P, TT])
        gap_exp1 = sb("gap_exp1", [P, TT])
        weight = sb("weight", [P, 2, TT])
        hit = sb("hit", [P, 2, TT, E])
        hit_w = sb("hit_w", [P, 2, TT, E])
        dispatch = sb("dispatch", [P, TT, E])
        left = sb("left", [P, 2, TT, E])
        dispatch_parts = sb("dispatch_parts", [P, TT, 3, E], BF16)
        dispatch_t = sb("dispatch_t", [3 * E, TOK], BF16)
        silu = [sb(f"silu{i}", [P, TOK]) for i in range(2)]
        hidden = [sb(f"hidden{i}", [P, TOK]) for i in range(2)]
        y_sb = sb("y_sb", [P, TT, D])

        psT = ctx.enter_context(nc.psum_tensor("m_psT", [P, DC, TOK], FP32))
        logits_ps = psT[:, 0, 0:TT * E].rearrange("p (t e) -> p t e", e=E)
        dispatch_ps = psT[0:3 * E, 1, 0:TOK // 2].bitcast(BF16)
        first_ps = [ctx.enter_context(nc.psum_tensor(f"first_ps{i}", [P, TOK], FP32)) for i in range(2)]
        second_ps = [ctx.enter_context(nc.psum_tensor(f"second_ps{i}", [P, TOK], FP32)) for i in range(2)]
        y_ps = ctx.enter_context(nc.psum_tensor("y_ps", [P, TT, D], FP32))

        weights_in, consts_set = sem("m_weights_in"), sem("m_consts_set")
        x_in = [sem("m_x_in0"), sem("m_x_in1")]
        x2_ready, stat_step, var_ready, rstd_ready, xn_ready = (
            sem(n) for n in ("x2_ready", "m_stat_step", "m_var_ready", "m_rstd_ready", "m_xn_ready"))
        xT_psum, xT_ready, logits_done, gate_step, gap_ready, gap_exp_ready = (
            sem(n) for n in ("m_xT_psum", "m_xT_ready", "logits_done", "gate_step", "gap_ready", "gap_exp_ready"))
        parts_ready, dispatch_psum, dispatch_ready = sem("parts_ready"), sem("dispatch_psum"), sem("dispatch_ready")
        unit_in, silu_ready, hidden_ready, unit_out = sem("unit_in"), sem("silu_ready"), sem("hidden_ready"), sem("unit_out")
        dve_passed, pe_passed = sem("m_dve_passed"), sem("m_pe_passed")
        y_ready, y_out = sem("y_ready"), sem("y_out")
        STAT_STEPS = 2 * TT
        GATE_STEPS = 12 + 2 * TT
        loads = (("ident", ident[:, :]), ("ident16", ident16[:, :]), ("select", select[:, :, :]), ("iota", iota[:, :, :]),
                 ("gate_t", gate[:, :, :]), ("w1_t", w1[:, :, :, :]), ("w2_t", w2[:, :, :]), ("sfc1_t", sfc1[:, :, :]),
                 ("sfc2_t", sfc2[:, :, :]), ("sfc3_t", sfc3[:, :, :]))

        with nc.Block() as block:
            @block.sync
            def _(sp):
                def load_x(b, par):
                    sp.dma_start(x_sb[:, par], io["x"][bass.ds(b, 1), par * TOK:(par + 1) * TOK, :].rearrange(
                        "o (t p) d -> p (o t) d", p=P)).then_inc(x_in[par], 16)

                def store_y(b, par):
                    sp.wait_ge(y_ready, b * 2 + par + 1)
                    sp.dma_start(io["out"][bass.ds(b, 1), par * TOK:(par + 1) * TOK, :].rearrange(
                        "o (t p) d -> p (o t) d", p=P), y_sb[:, :, :]).then_inc(y_out, 16)

                load_x(0, 0)
                load_x(0, 1)
                for name, dst in loads:
                    src = io[name]
                    if name in ("gate_t", "sfc1_t", "sfc2_t", "sfc3_t"):
                        src = src.rearrange("(c p) n -> p c n", p=P)
                    elif name == "w1_t":
                        src = src.rearrange("e (c p) f -> p c e f", p=P)
                        for c in range(DC):
                            sp.dma_start(dst[:, c], src[:, c]).then_inc(weights_in, 16)
                        continue
                    elif name == "w2_t":
                        src = src.rearrange("e f d -> f e d")
                    sp.dma_start(dst, src).then_inc(weights_in, 16)
                with sp.Fori(0, B - 1) as b:
                    for par in range(2):
                        sp.wait_ge(x2_ready, b * 2 + par + 1)
                        load_x(b + 1, par)
                        store_y(b, par)
                for par in range(2):
                    store_y(B - 1, par)
                sp.wait_ge(y_out, GROUPS * 16)

            @block.gpsimd
            def _(pool):
                nc.gpsimd.memset(minus_half[:, :], -0.5).then_inc(consts_set, 1)
                pool.wait_ge(consts_set, 1)
                with pool.Fori(0, GROUPS) as g:
                    pool.wait_ge(var_ready, g + 1)
                    nc.gpsimd.tensor_tensor(rstd[:, :], var_eps[:, :], minus_half[:, :], ALU.pow).then_inc(rstd_ready, 1)

            @block.vector
            def _(dve):
                dve.wait_ge(weights_in, (len(loads) + 1) * 16)
                with dve.Fori(0, B) as b:
                    for par in range(2):
                        g = b * 2 + par
                        steps = [0]

                        def step(ins):
                            steps[0] += 1
                            ins.then_inc(gate_step, 1)

                        def settle():
                            wait_apart(dve, gate_step, g * GATE_STEPS + steps[0], dve_passed)

                        dve.wait_ge(x_in[par], b * 16 + 16)
                        for t in range(TT):
                            att = ctx_all[:, bass.ds(b * H, H), par * TT + t, :]
                            ins = nc.vector.tensor_tensor(x2[:, par, t].rearrange("p (h d) -> p h d", d=DH),
                                                          x_sb[:, par, t].rearrange("p (h d) -> p h d", d=DH), att, ALU.add)
                        ins.then_inc(x2_ready, 1)
                        dve.wait_ge(x2_ready, g + 1)
                        for t in range(TT):
                            nc.vector.bn_stats(stats[:, t], x2[:, par, t]).then_inc(stat_step, 1)
                        for t in range(TT):
                            wait_apart(dve, stat_step, g * STAT_STEPS + t + 1, dve_passed)
                            nc.vector.bn_aggr(moments[:, t], stats[:, t]).then_inc(stat_step, 1)
                        dve.wait_ge(stat_step, (g + 1) * STAT_STEPS)
                        nc.vector.tensor_scalar(var_eps[:, :], moments[:, :, 1], EPS, None, ALU.add).then_inc(var_ready, 1)
                        dve.wait_ge(rstd_ready, g + 1)
                        dve.wait_ge(xT_psum, g)
                        for t in range(TT):
                            ins = nc.vector.tensor_scalar(xn[:, t], x2[:, par, t], moments[:, t, 0:1], rstd[:, t:t + 1],
                                                          ALU.subtract, ALU.mult)
                        ins.then_inc(xn_ready, 1)

                        dve.wait_ge(logits_done, g + 1)
                        step(nc.vector.tensor_copy(logits[:, :, :], logits_ps))
                        settle()
                        for t in range(TT):
                            step(nc.vector.max(top[:, t], logits[:, t]))
                        settle()
                        for t in range(TT):
                            step(nc.vector.max_index(top_at[:, t], top[:, t], logits[:, t]))
                        nc.vector.tensor_tensor(gap[:, :], top[:, :, 1], top[:, :, 0], ALU.subtract).then_inc(gap_ready, 1)
                        settle()
                        step(nc.vector.tensor_copy(top_atf[:, :, :], top_at[:, :, 0:2]))
                        dve.wait_ge(gap_exp_ready, g + 1)
                        step(nc.vector.tensor_scalar(gap_exp1[:, :], gap_exp[:, :], 1.0, None, ALU.add))
                        settle()
                        step(nc.vector.reciprocal(weight[:, 0], gap_exp1[:, :]))
                        settle()
                        step(nc.vector.tensor_tensor(weight[:, 1], weight[:, 0], gap_exp[:, :], ALU.mult))
                        for i in range(2):
                            step(nc.vector.tensor_tensor(hit[:, i], iota[:, :, :],
                                                         top_atf[:, :, i:i + 1].to_broadcast([P, TT, E]), ALU.is_equal))
                        settle()
                        for i in range(2):
                            step(nc.vector.tensor_tensor(hit_w[:, i], hit[:, i],
                                                         weight[:, i, :, None].to_broadcast([P, TT, E]), ALU.mult))
                        settle()
                        step(nc.vector.tensor_tensor(dispatch[:, :, :], hit_w[:, 0], hit_w[:, 1], ALU.add))
                        settle()
                        dve.wait_ge(dispatch_psum, g)
                        step(nc.vector.tensor_copy(dispatch_parts[:, :, 0, :], dispatch[:, :, :]))
                        settle()
                        step(nc.vector.tensor_tensor(left[:, 0], dispatch[:, :, :], dispatch_parts[:, :, 0, :], ALU.subtract))
                        settle()
                        nc.vector.tensor_copy(dispatch_parts[:, :, 1, :], left[:, 0]).then_inc(parts_ready, 1)
                        dve.wait_ge(parts_ready, g * 3 + 1)
                        nc.vector.tensor_tensor(left[:, 1], left[:, 0], dispatch_parts[:, :, 1, :], ALU.subtract).then_inc(parts_ready, 1)
                        dve.wait_ge(parts_ready, g * 3 + 2)
                        nc.vector.tensor_copy(dispatch_parts[:, :, 2, :], left[:, 1]).then_inc(parts_ready, 1)
                        assert steps[0] == GATE_STEPS, steps

                        for u in range(UNITS):
                            n = g * UNITS + u
                            dve.wait_ge(silu_ready, n + 1)
                            if u >= 2:
                                dve.wait_ge(unit_out, n - 1)
                            else:
                                dve.wait_ge(unit_out, g * UNITS)
                            nc.vector.tensor_tensor(hidden[u % 2][:, :], second_ps[u % 2][:, :], silu[u % 2][:, :], ALU.mult
                                                    ).then_inc(hidden_ready, 1)
                        dve.wait_ge(unit_out, (g + 1) * UNITS)
                        dve.wait_ge(y_out, g * 16)
                        nc.vector.tensor_tensor(y_sb[:, :, :], y_ps[:, :, :], x2[:, par], ALU.add).then_inc(y_ready, 1)

            @block.tensor
            def _(pe):
                pe.wait_ge(weights_in, (len(loads) + 1) * 16)

                def unit_products(g, u):
                    n = g * UNITS + u
                    if u >= 2:
                        pe.wait_ge(hidden_ready, n - 1)
                    else:
                        pe.wait_ge(hidden_ready, g * UNITS)
                    for c in range(DC):
                        w = sfc1[:, c, u * P:(u + 1) * P] if u < SU else w1[:, c, u - SU, :]
                        nc.tensor.matmul(first_ps[u % 2][:, :], w, xT[:, c, :], start=c == 0, stop=c == DC - 1)
                    if u < SU:
                        for c in range(DC):
                            ins = nc.tensor.matmul(second_ps[u % 2][:, :], sfc2[:, c, u * P:(u + 1) * P], xT[:, c, :],
                                                   start=c == 0, stop=c == DC - 1)
                    else:
                        ins = nc.tensor.matmul(second_ps[u % 2][:, :], select[:, u - SU, :], dispatch_t[:, :], start=True, stop=True)
                    ins.then_inc(unit_in, 1)

                def unit_output(g, u):
                    pe.wait_ge(hidden_ready, g * UNITS + u + 1)
                    if u == 0:
                        pe.wait_ge(y_ready, g)
                    w = sfc3[:, u, :] if u < SU else w2[:, u - SU, :]
                    for t in range(TT):
                        ins = nc.tensor.matmul(y_ps[:, t, :], hidden[u % 2][:, t * P:(t + 1) * P], w,
                                               start=u == 0 and t % 2 == 0, stop=u == UNITS - 1, skip_group_check=True)
                    ins.then_inc(unit_out, 1)

                with pe.Fori(0, GROUPS) as g:
                    pe.wait_ge(xn_ready, g + 1)
                    pe.wait_ge(dispatch_ready, g)
                    for c in range(DC):
                        for t in range(TT):
                            ins = nc.tensor.transpose(psT[:, c, t * P:(t + 1) * P], xn[:, t, c * P:(c + 1) * P], ident[:, :])
                    ins.then_inc(xT_psum, 1)
                    pe.wait_ge(xT_ready, g + 1)
                    for t in range(TT):
                        for c in range(DC):
                            ins = nc.tensor.matmul(logits_ps[:, t, :], xT[:, c, t * P:(t + 1) * P], gate[:, c, :],
                                                   start=c == 0, stop=c == DC - 1)
                    ins.then_inc(logits_done, 1)
                    for u in range(UNITS):
                        if u == SU:
                            wait_apart(pe, parts_ready, (g + 1) * 3, pe_passed)
                            for t in range(TT):
                                ins = nc.tensor.transpose(dispatch_ps[:, t * P:(t + 1) * P],
                                                          dispatch_parts[:, t].rearrange("p a e -> p (a e)"), ident16[:, :])
                            ins.then_inc(dispatch_psum, 1)
                            pe.wait_ge(dispatch_ready, g + 1)
                        unit_products(g, u)
                        if u >= 1:
                            unit_output(g, u - 1)
                    unit_output(g, UNITS - 1)

            @block.scalar
            def _(act):
                with act.Fori(0, GROUPS) as g:
                    act.wait_ge(xT_psum, g + 1)
                    act.wait_ge(unit_in, g * UNITS)
                    nc.scalar.activation(xT[:, :, :], psT[:, :, :], ACT.Copy).then_inc(xT_ready, 1)
                    act.wait_ge(gap_ready, g + 1)
                    nc.scalar.activation(gap_exp[:, :], gap[:, :], ACT.Exp).then_inc(gap_exp_ready, 1)
                    for u in range(UNITS):
                        n = g * UNITS + u
                        if u == SU:
                            act.wait_ge(dispatch_psum, g + 1)
                            nc.scalar.activation(dispatch_t[:, :], dispatch_ps, ACT.Copy).then_inc(dispatch_ready, 1)
                        act.wait_ge(unit_in, n + 1)
                        if u >= 2:
                            act.wait_ge(hidden_ready, n - 1)
                        else:
                            act.wait_ge(hidden_ready, g * UNITS)
                        nc.scalar.activation(silu[u % 2][:, :], first_ps[u % 2][:, :], ACT.Silu).then_inc(silu_ready, 1)


def build(nc, io, phases=("project", "position", "attend", "mix")):
    scratch = {
        "q_a": nc.dram_tensor("q_a", [len(PART_A), BH, DH, S], BF16).ap(),
        "k_a": nc.dram_tensor("k_a", [len(PART_A), BH, DH, S], BF16).ap(),
        "k_b": nc.dram_tensor("k_b", [len(PART_B), BH, DH, S], BF16).ap(),
        "q_blocks": nc.dram_tensor("q_blocks", [S // HQ, ROWS, BH, HQ], BF16).ap(),
        "tables": nc.dram_tensor("tables", [2, ROWS, TABLE], BF16).ap(),
        "v": nc.dram_tensor("v_all", [B, P, KT, D], FP32).ap(),
        "z": [nc.dram_tensor(f"z_all{i}", [BH, S // 2, S], FP32).ap() for i in range(2)],
    }
    project(nc, io, scratch)
    reblock_queries(nc, scratch)
    position(nc, scratch)
    with nc.sbuf_tensor("ctx_all", [P, BH, KT, DH], FP32) as ctx_all:
        attend(nc, io, scratch, ctx_all)
        mix(nc, io, ctx_all)


def kernel(L0_attn_hidden_states, L0_attn_Wq, L0_attn_bq, L0_attn_Wk, L0_attn_bk, L0_attn_Wv, L0_attn_bv,
           L0_attn_dist_emb, L0_ffn_gate_w, L0_ffn_w1, L0_ffn_w2, L0_ffn_sfc1, L0_ffn_sfc2, L0_ffn_sfc3):
    import ml_dtypes
    import concourse.bacc as bacc
    from concourse.bass_utils import run_bass_kernel_spmd

    select = np.zeros((3, E, E, P), ml_dtypes.bfloat16)
    for e in range(E):
        select[:, e, e, :] = 1
    dist = np.asarray(L0_attn_dist_emb).T
    arrays = {
        "x": L0_attn_hidden_states, "bq": L0_attn_bq, "bk": L0_attn_bk, "bv": L0_attn_bv,
        "wq_t": np.asarray(L0_attn_Wq).T, "wk_t": np.asarray(L0_attn_Wk).T, "wv_t": np.asarray(L0_attn_Wv).T,
        "dist_t": dist, "dist_rev": dist[:, ::-1],
        "gate_t": np.asarray(L0_ffn_gate_w).T, "w1_t": np.asarray(L0_ffn_w1).transpose(0, 2, 1),
        "w2_t": np.asarray(L0_ffn_w2).transpose(0, 2, 1), "sfc1_t": np.asarray(L0_ffn_sfc1).T,
        "sfc2_t": np.asarray(L0_ffn_sfc2).T, "sfc3_t": np.asarray(L0_ffn_sfc3).T,
        "ident": np.eye(P, dtype=np.float32), "ident16": np.eye(P, dtype=ml_dtypes.bfloat16),
        "select": select.reshape(3 * E, E, P),
        "iota": np.broadcast_to(np.arange(E, dtype=np.float32), (P, TT, E)),
    }
    nc = bacc.Bacc("TRN2", target_bir_lowering=False, num_devices=1)
    io, in_map = {}, {}
    for name, a in arrays.items():
        a = np.ascontiguousarray(a)
        in_map[f"in_{name}"] = a
        io[name] = nc.dram_tensor(f"in_{name}", a.shape, mybir.dt.from_np(a.dtype), kind="ExternalInput").ap()
    io["out"] = nc.dram_tensor("out_x", [B, S, D], FP32, kind="ExternalOutput").ap()
    build(nc, io)
    return run_bass_kernel_spmd(nc, [in_map], core_ids=[0]).results[0]["out_x"]
```

```python
from contextlib import ExitStack

import numpy as np

import concourse.bass as bass
from concourse import mybir
from concourse.alu_op_type import AluOpType as ALU

FP32 = mybir.dt.float32
BF16 = mybir.dt.bfloat16
U32 = mybir.dt.uint32
ACT = mybir.ActivationFunctionType
AXIS = mybir.AxisListType

P = 128
B, S, D = 8, 1024, 256
H, DH = 16, 16
BH = B * H
HG = H // 2
E, F = 16, 128
SH = 512
MAX_POS = 512
TABLE = 2 * S
EPS = 1e-5
DC = D // P
TOK = 512
TT = TOK // P
GROUPS = B * S // TOK
KT = S // P
PART_A = (0, 0, 0, 1, 1, 2)
PART_B = (0, 1, 2, 0, 1, 0)
ROWS = len(PART_A) * DH
HQ = 64
HK = HQ
WIN = HQ + P - 1


def wait_count(engine, semaphore, count):
    if not (isinstance(count, int) and count <= 0):
        engine.wait_ge(semaphore, count)


def wait_apart(engine, semaphore, count, passed):
    wait_count(engine, semaphore, count)
    if not isinstance(count, int):
        engine.sem_inc(passed, 1)


def _bank_pair(ctx, nc, name):
    return ctx.enter_context(nc.psum_tensor(name, [P, 2, 512], FP32))


def project(nc, io, scratch):
    with ExitStack() as ctx:
        def sb(name, shape, dt=FP32):
            return ctx.enter_context(nc.sbuf_tensor(name, shape, dt))

        def sem(name):
            return ctx.enter_context(nc.semaphore(name))

        ident = sb("p_ident", [P, P])
        wq, wk, wv = (sb(n, [P, DC, D]) for n in ("wq_sb", "wk_sb", "wv_sb"))
        bias_q, bias_k, bias_k4 = (sb(n, [P, DC]) for n in ("bias_q", "bias_k", "bias_k4"))
        bias_v = sb("bias_v", [P, D])
        minus_half = sb("p_minus_half", [P, TT])
        x_sb = sb("p_x", [P, 2, TT, D])
        xn = sb("p_xn", [P, 2, TT, D])
        stats = sb("p_stats", [P, 2, TT, 6])
        moments = sb("p_moments", [P, 2, TT, 2])
        var_eps = sb("p_var_eps", [P, 2, TT])
        rstd = sb("p_rstd", [P, 2, TT])
        xT = sb("p_xT", [P, 2, DC, TOK])
        qk32 = sb("qk32", [P, 4 * TOK])
        rest = sb("rest", [P, 4 * TOK])
        parts = sb("parts", [P, 2, 3, 4, TOK], BF16)
        v_sb = sb("p_v", [P, 2, TT, D])
        table = sb("table", [DH, 2, TABLE])
        table_parts = sb("table_parts", [DH, 3, 2, TABLE], BF16)

        psT = ctx.enter_context(nc.psum_tensor("p_psT", [P, DC, TOK], FP32))
        psQK = ctx.enter_context(nc.psum_tensor("psQK", [P, 4, TOK], FP32))
        psV = ctx.enter_context(nc.psum_tensor("psV", [P, TT, D], FP32))

        weights_in, table_in, tables_out = sem("weights_in"), sem("table_in"), sem("tables_out")
        x_in = [sem("x_in0"), sem("x_in1")]
        consts_set, table_step, part_cut, bias_set = sem("consts_set"), sem("table_step"), sem("part_cut"), sem("bias_set")
        stat_step, var_ready, rstd_ready, xn_ready = sem("stat_step"), sem("var_ready"), sem("rstd_ready"), sem("xn_ready")
        xT_psum, xT_ready, qk_psum, v_psum = sem("xT_psum"), sem("xT_ready"), sem("qk_psum"), sem("v_psum")
        qk32_ready, part1, rest1, part2, rest2, part3 = (
            sem(n) for n in ("qk32_ready", "part1", "rest1", "part2", "rest2", "part3"))
        v_ready = sem("v_ready")
        dve_passed, pool_passed = sem("p_dve_passed"), sem("p_pool_passed")
        stored = [sem("stored0"), sem("stored1")]
        STORES = 3 * 6 + 1

        with nc.Block() as block:
            @block.sync
            def _(sp):
                sp.dma_start(ident[:, :], io["ident"]).then_inc(weights_in, 16)
                for w, name in ((wq, "wq_t"), (wk, "wk_t"), (wv, "wv_t")):
                    sp.dma_start(w[:, :, :], io[name].rearrange("(c p) n -> p c n", p=P)).then_inc(weights_in, 16)
                for bias, name in ((bias_q, "bq"), (bias_k, "bk")):
                    with nc.allow_non_contiguous_dma(reason="256 biases, once"):
                        sp.dma_start(bias[:, :], io[name].rearrange("(c p) -> p c", p=P)).then_inc(weights_in, 16)
                sp.dma_start(bias_v[:, :], io["bv"].rearrange("(a n) -> a n", a=1).to_broadcast([P, D])).then_inc(weights_in, 16)
                low = S - MAX_POS
                n = 2 * MAX_POS - 1
                sp.dma_start(table[:, 1, 0:low], io["dist_t"][:, n - low:n]).then_inc(table_in, 16)
                sp.dma_start(table[:, 1, low:low + n], io["dist_t"]).then_inc(table_in, 16)
                sp.dma_start(table[:, 0, S - MAX_POS:S - MAX_POS + n], io["dist_rev"]).then_inc(table_in, 16)
                sp.dma_start(table[:, 0, S - MAX_POS + n:S - MAX_POS + n + low], io["dist_rev"][:, 0:low]).then_inc(table_in, 16)
                sp.wait_ge(part_cut, 3)
                for g, part in enumerate(PART_B):
                    for way in range(2):
                        sp.dma_start(scratch["tables"][way, g * DH:(g + 1) * DH, :],
                                     table_parts[:, part, way, :]).then_inc(tables_out, 16)

                def load_x(b, par):
                    sp.dma_start(x_sb[:, par], io["x"][bass.ds(b, 1), par * TOK:(par + 1) * TOK, :].rearrange(
                        "o (t p) d -> p (o t) d", p=P)).then_inc(x_in[par], 16)

                def store(b, par):
                    g = b * 2 + par
                    sp.wait_ge(v_ready, g + 1)
                    sp.dma_start(scratch["v"][bass.ds(b, 1), :, par * TT:(par + 1) * TT, :].rearrange("o p t n -> p (o t) n"),
                                 v_sb[:, par]).then_inc(stored[par], 16)
                    sp.wait_ge(part2, g + 1)
                    sp.wait_ge(part3, g + 1)
                    for part in range(3):
                        for rows, first in (("q_rows", 0), ("k_rows", 2)):
                            dst = scratch[rows][part, bass.ds(b * 2, 2), :, :, par * TOK:(par + 1) * TOK]
                            sp.dma_start(dst.rearrange("g d h s -> (d h) g s"),
                                         parts[:, par, part, first:first + 2, :]).then_inc(stored[par], 16)
                        for tiles, first in (("q_tiles", 0), ("k_tiles", 2)):
                            for half in range(2):
                                dst = scratch[tiles][part, par * TOK // HK:(par + 1) * TOK // HK, bass.ds(b * 2 + half, 1)]
                                sp.dma_start(dst.rearrange("t g d h s -> (d h) (t g) s"),
                                             parts[:, par, part, first + half, :].rearrange("p (t s) -> p t s", s=HK)
                                             ).then_inc(stored[par], 16)

                load_x(0, 0)
                load_x(0, 1)
                with sp.Fori(0, B - 1) as b:
                    for par in range(2):
                        sp.wait_ge(xn_ready, b * 2 + par + 1)
                        load_x(b + 1, par)
                        store(b, par)
                for par in range(2):
                    store(B - 1, par)
                for par in range(2):
                    sp.wait_ge(stored[par], B * STORES * 16)
                sp.wait_ge(tables_out, 16 * 2 * len(PART_B))

            @block.gpsimd
            def _(pool):
                nc.gpsimd.memset(minus_half[:, :], -0.5).then_inc(consts_set, 1)
                pool.wait_ge(consts_set, 1)
                with pool.Fori(0, B) as b:
                    for par in range(2):
                        g = b * 2 + par
                        pool.wait_ge(var_ready, g + 1)
                        nc.gpsimd.tensor_tensor(rstd[:, par], var_eps[:, par], minus_half[:, :], ALU.pow).then_inc(rstd_ready, 1)
                        wait_apart(pool, rest1, g + 1, pool_passed)
                        nc.gpsimd.tensor_copy(parts[:, par, 1].rearrange("p a t -> p (a t)"), rest[:, :]).then_inc(part2, 1)
                        wait_apart(pool, rest2, g + 1, pool_passed)
                        nc.gpsimd.tensor_copy(parts[:, par, 2].rearrange("p a t -> p (a t)"), rest[:, :]).then_inc(part3, 1)

            @block.vector
            def _(dve):
                dve.wait_ge(table_in, 64)
                n = 2 * MAX_POS - 1
                end = S - MAX_POS + n
                nc.vector.tensor_copy(table[:, 1, end:TABLE], table[:, 1, end - 1:end].to_broadcast([DH, TABLE - end])).then_inc(table_step, 1)
                first = S - MAX_POS
                nc.vector.tensor_copy(table[:, 0, 0:first], table[:, 0, first:first + 1].to_broadcast([DH, first])).then_inc(table_step, 1)
                nc.vector.memset(table[:, 0, TABLE - 1:TABLE], 0.0).then_inc(table_step, 1)
                dve.wait_ge(table_step, 3)
                nc.vector.tensor_scalar(table[:, 0, :], table[:, 0, :], -1.0, None, ALU.mult).then_inc(table_step, 1)
                nc.vector.tensor_scalar(table[:, 1, :], table[:, 1, :], 4.0, None, ALU.mult).then_inc(table_step, 1)
                for part in range(3):
                    dve.wait_ge(table_step, 5 + part)
                    ins = nc.vector.tensor_copy(table_parts[:, part], table[:, :, :])
                    ins.then_inc(part_cut, 1)
                    if part < 2:
                        dve.wait_ge(part_cut, part + 1)
                        nc.vector.tensor_tensor(table[:, :, :], table[:, :, :], table_parts[:, part], ALU.subtract).then_inc(table_step, 1)
                dve.wait_ge(weights_in, 7 * 16)
                nc.vector.tensor_scalar(bias_k4[:, :], bias_k[:, :], -0.25, None, ALU.mult).then_inc(bias_set, 1)
                with dve.Fori(0, B) as b:
                    for par in range(2):
                        g = b * 2 + par
                        dve.wait_ge(x_in[par], b * 16 + 16)
                        for t in range(TT):
                            nc.vector.bn_stats(stats[:, par, t], x_sb[:, par, t]).then_inc(stat_step, 1)
                        for t in range(TT):
                            wait_apart(dve, stat_step, g * 2 * TT + t + 1, dve_passed)
                            nc.vector.bn_aggr(moments[:, par, t], stats[:, par, t]).then_inc(stat_step, 1)
                        dve.wait_ge(stat_step, g * 2 * TT + 2 * TT)
                        nc.vector.tensor_scalar(var_eps[:, par], moments[:, par, :, 1], EPS, None, ALU.add).then_inc(var_ready, 1)
                        dve.wait_ge(rstd_ready, g + 1)
                        for t in range(TT):
                            ins = nc.vector.tensor_scalar(xn[:, par, t], x_sb[:, par, t], moments[:, par, t, 0:1],
                                                          rstd[:, par, t:t + 1], ALU.subtract, ALU.mult)
                        ins.then_inc(xn_ready, 1)
                        dve.wait_ge(part1, g + 1)
                        dve.wait_ge(part3, g)
                        nc.vector.tensor_tensor(rest[:, :], qk32[:, :], parts[:, par, 0].rearrange("p a t -> p (a t)"),
                                                ALU.subtract).then_inc(rest1, 1)
                        dve.wait_ge(v_psum, g + 1)
                        dve.wait_ge(stored[par], b * STORES * 16)
                        nc.vector.tensor_tensor(v_sb[:, par], psV[:, :, :], bias_v[:, None, :].to_broadcast([P, TT, D]),
                                                ALU.add).then_inc(v_ready, 1)
                        dve.wait_ge(part2, g + 1)
                        nc.vector.tensor_tensor(rest[:, :], rest[:, :], parts[:, par, 1].rearrange("p a t -> p (a t)"),
                                                ALU.subtract).then_inc(rest2, 1)

            @block.tensor
            def _(pe):
                pe.wait_ge(weights_in, 7 * 16)
                with pe.Fori(0, B) as b:
                    for par in range(2):
                        g = b * 2 + par
                        pe.wait_ge(xn_ready, g + 1)
                        for c in range(DC):
                            for t in range(TT):
                                ins = nc.tensor.transpose(psT[:, c, t * P:(t + 1) * P], xn[:, par, t, c * P:(c + 1) * P], ident[:, :])
                        ins.then_inc(xT_psum, 1)
                        pe.wait_ge(xT_ready, g + 1)
                        pe.wait_ge(qk32_ready, g * 4)
                        for slot in range(4):
                            w, half = (wq, wk)[slot // 2], slot % 2
                            for c in range(DC):
                                ins = nc.tensor.matmul(psQK[:, slot, :], w[:, c, half * P:(half + 1) * P], xT[:, par, c, :],
                                                       start=c == 0, stop=c == DC - 1)
                            ins.then_inc(qk_psum, 1)
                        pe.wait_ge(v_ready, g)
                        for t in range(TT):
                            for c in range(DC):
                                ins = nc.tensor.matmul(psV[:, t, :], xT[:, par, c, t * P:(t + 1) * P], wv[:, c, :],
                                                       start=c == 0, stop=c == DC - 1)
                        ins.then_inc(v_psum, 1)

            @block.scalar
            def _(act):
                act.wait_ge(weights_in, 7 * 16)
                act.wait_ge(bias_set, 1)
                with act.Fori(0, B) as b:
                    for par in range(2):
                        g = b * 2 + par
                        act.wait_ge(xT_psum, g + 1)
                        nc.scalar.activation(xT[:, par], psT[:, :, :], ACT.Copy).then_inc(xT_ready, 1)
                        act.wait_ge(rest1, g)
                        for slot in range(4):
                            bias, scale = ((bias_q, 1.0), (bias_k4, -0.25))[slot // 2]
                            act.wait_ge(qk_psum, g * 4 + slot + 1)
                            nc.scalar.activation(qk32[:, slot * TOK:(slot + 1) * TOK], psQK[:, slot, :], ACT.Identity,
                                                 bias=bias[:, slot % 2:slot % 2 + 1], scale=scale).then_inc(qk32_ready, 1)
                        act.wait_ge(qk32_ready, g * 4 + 4)
                        act.wait_ge(stored[par], b * STORES * 16)
                        nc.scalar.activation(parts[:, par, 0].rearrange("p a t -> p (a t)"), qk32[:, :], ACT.Copy).then_inc(part1, 1)


def position(nc, scratch):
    PER_BLOCK = 4
    QQ = S // (HQ * PER_BLOCK)
    BLOCKS = QQ * KT
    STEPS = 8
    ORDER = [("query", 0), ("query", 1)] + [("key", step) for step in range(STEPS // 2)]
    for step in range(STEPS // 2):
        ORDER += [("query", step + 2), ("key", step + STEPS // 2)]
    ORDER += [("query", step) for step in range(STEPS // 2 + 2, STEPS)]
    QS, KS = HQ // STEPS, P // STEPS
    PARTS = 4
    PQ = HQ // PARTS
    GROUPS6 = len(PART_A)
    with ExitStack() as ctx:
        def sb(name, shape, dt=FP32):
            return ctx.enter_context(nc.sbuf_tensor(name, shape, dt))

        def sem(name):
            return ctx.enter_context(nc.semaphore(name))

        queries = [sb(f"queries{h}", [ROWS, BH, HQ], BF16) for h in range(PER_BLOCK)]
        keys = sb("keys", [ROWS, 2, BH, HK], BF16)
        falling = [sb(f"falling{i}", [ROWS, WIN], BF16) for i in range(2)]
        rising = [sb(f"rising{i}", [ROWS, WIN], BF16) for i in range(2)]
        z = [sb(f"z{i}", [P, HQ, P]) for i in range(2)]
        q_ps = [_bank_pair(ctx, nc, f"q_ps{i}") for i in range(2)]
        k_ps = [_bank_pair(ctx, nc, f"k_ps{i}") for i in range(2)]

        keys_in = [sem(f"keys_in{half}") for half in range(2)]
        queries_in = [sem(f"queries_in{h}") for h in range(PER_BLOCK)]
        falling_in = [sem(f"falling_in{i}") for i in range(2)]
        rising_in = [sem(f"rising_in{i}") for i in range(2)]
        z_out = [[sem(f"z_out{i}_{part}") for part in range(PARTS)] for i in range(2)]
        pe_passed, sp_passed = sem("z_pe_passed"), sem("z_sp_passed")
        q_terms, q_copied, k_terms, k_added = sem("q_terms"), sem("q_copied"), sem("k_terms"), sem("k_added")

        with nc.Block() as block:
            @block.sync
            def _(sp):
                def load_queries(qq, h):
                    for g in range(GROUPS6):
                        sp.dma_start(queries[h][g * DH:(g + 1) * DH, :, :].rearrange("d (g h) s -> d g (h s)", h=HG),
                                     scratch["q_tiles"][PART_A[g], qq * PER_BLOCK + h].rearrange("g d h s -> d g (h s)")
                                     ).then_inc(queries_in[h], 16)

                def load_keys(kt, half):
                    for g in range(GROUPS6):
                        sp.dma_start(keys[g * DH:(g + 1) * DH, half].rearrange("d (g h) s -> d g (h s)", h=HG),
                                     scratch["k_tiles"][PART_A[g], bass.ds(kt * 2 + half, 1)].rearrange("o g d h s -> d (o g) (h s)")
                                     ).then_inc(keys_in[half], 16)

                def load_falling(qq, kt, h):
                    sp.dma_start(falling[h % 2][:, :], scratch["tables"][0, :, bass.ds(kt * P + (S - HQ - (qq * PER_BLOCK + h) * HQ), WIN)]
                                 ).then_inc(falling_in[h % 2], 16)

                def load_rising(qq, kt, h):
                    sp.dma_start(rising[h % 2][:, :], scratch["tables"][1, :, bass.ds((S - P + (qq * PER_BLOCK + h) * HQ) - kt * P, WIN)]
                                 ).then_inc(rising_in[h % 2], 16)

                def block_of(qq, kt, nxt, last=False):
                    for h in range(PER_BLOCK):
                        m = (kt + qq * KT) * PER_BLOCK + h
                        if h == PER_BLOCK - 1 and not last:
                            for half in range(2):
                                wait_apart(sp, k_terms, m * STEPS + (half + 1) * STEPS // 2, sp_passed)
                                load_keys(nxt[1], half)
                        wait_apart(sp, k_added, (m + 1) * STEPS, sp_passed)
                        for part in range(PARTS):
                            first = qq * PER_BLOCK * HQ + h * HQ + part * PQ
                            sp.dma_start(scratch["z"][first // (S // 2)][:, first % (S // 2):first % (S // 2) + PQ, bass.ds(kt * P, P)],
                                         z[h % 2][:, part * PQ:(part + 1) * PQ, :]).then_inc(z_out[h % 2][part], 16)
                        load_rising(*((qq, kt) if h < 2 else nxt), (h + 2) % PER_BLOCK)
                        wait_apart(sp, q_terms, (m + 2) * STEPS, sp_passed)
                        load_falling(*((qq, kt) if h < 1 else nxt), (h + 3) % PER_BLOCK)
                        if nxt[0] == qq + 1:
                            for j in ((0, 1), (2,), (3,), ())[h]:
                                load_queries(qq + 1, j)

                for h in range(2):
                    load_queries(0, h)
                    load_falling(0, 0, h)
                    load_rising(0, 0, h)
                for half in range(2):
                    load_keys(0, half)
                for h in range(2, PER_BLOCK):
                    load_queries(0, h)
                sp.wait_ge(q_terms, STEPS)
                load_falling(0, 0, 2)
                for qq in range(QQ):
                    with sp.Fori(0, KT - 1) as kt:
                        block_of(qq, kt, (qq, kt + 1))
                    block_of(qq, KT - 1, (qq + 1, 0) if qq < QQ - 1 else (0, 0), last=qq == QQ - 1)
                for i in range(2):
                    for part in range(PARTS):
                        sp.wait_ge(z_out[i][part], BLOCKS * PER_BLOCK // 2 * 16)
                    sp.wait_ge(falling_in[i], (BLOCKS * PER_BLOCK // 2 + 2 - i) * 16)
                    sp.wait_ge(rising_in[i], (BLOCKS * PER_BLOCK // 2 + 1) * 16)

            @block.tensor
            def _(pe):
                def query_terms(m, h, step):
                    wait_count(pe, q_copied, m * STEPS + step - 1)
                    for i in range(QS):
                        q = step * QS + i
                        ins = nc.tensor.matmul(q_ps[step % 2][:, i // 4, (i % 4) * P:(i % 4 + 1) * P], queries[h][:, :, q],
                                               falling[h % 2][:, HQ - 1 - q:HQ - 1 - q + P], start=True, stop=True)
                    ins.then_inc(q_terms, 1)

                def key_terms(m, h, step):
                    pe.wait_ge(k_added, m * STEPS + max(step - 1, 0))
                    for i in range(KS):
                        k = step * KS + i
                        ins = nc.tensor.matmul(k_ps[step % 2][:, i // 8, (i % 8) * HQ:(i % 8 + 1) * HQ], keys[:, k // HK, :, k % HK],
                                               rising[h % 2][:, P - 1 - k:P - 1 - k + HQ], start=True, stop=True)
                    ins.then_inc(k_terms, 1)

                pe.wait_ge(queries_in[0], GROUPS6 * 16)
                pe.wait_ge(falling_in[0], 16)
                for step in range(STEPS):
                    query_terms(0, 0, step)
                with pe.Fori(0, BLOCKS) as n:
                    for h in range(PER_BLOCK):
                        m = n * PER_BLOCK + h
                        pe.wait_ge(rising_in[h % 2], (n * 2 + h // 2 + 1) * 16)
                        pe.wait_ge(falling_in[(h + 1) % 2], (n * 2 + (h + 1) // 2 + 1) * 16)
                        quarter = n // KT if h < PER_BLOCK - 1 else ((n + 1) % BLOCKS) // KT
                        pe.wait_ge(queries_in[(h + 1) % PER_BLOCK], (quarter + 1) * GROUPS6 * 16)
                        for kind, step in ORDER:
                            if kind == "query":
                                query_terms(m + 1, (h + 1) % PER_BLOCK, step)
                            else:
                                if h == 0 and step % (STEPS // 2) == 0:
                                    pe.wait_ge(keys_in[step // (STEPS // 2)], (n + 1) * GROUPS6 * 16)
                                key_terms(m, h, step)

            @block.scalar
            def _(act):
                def copy(m, h, step):
                    act.wait_ge(q_terms, m * STEPS + step + 1)
                    nc.scalar.activation(z[h % 2][:, step * QS:(step + 1) * QS, :],
                                         q_ps[step % 2][:, :, :].rearrange("p a (q k) -> p (a q) k", k=P), ACT.Copy).then_inc(q_copied, 1)

                for step in range(STEPS):
                    copy(0, 0, step)
                with act.Fori(0, BLOCKS) as n:
                    for h in range(PER_BLOCK):
                        for step in range(STEPS):
                            if step % (STEPS // PARTS) == 0:
                                act.wait_ge(z_out[(h + 1) % 2][step // (STEPS // PARTS)], (n * 2 + (h + 1) // 2) * 16)
                            copy(n * PER_BLOCK + h + 1, (h + 1) % PER_BLOCK, step)

            @block.vector
            def _(dve):
                with dve.Fori(0, BLOCKS) as n:
                    for h in range(PER_BLOCK):
                        m = n * PER_BLOCK + h
                        dve.wait_ge(q_copied, (m + 1) * STEPS)
                        for step in range(STEPS):
                            dve.wait_ge(k_terms, m * STEPS + step + 1)
                            part = z[h % 2][:, :, step * KS:(step + 1) * KS].rearrange("p q k -> p k q")
                            nc.vector.tensor_tensor(part, k_ps[step % 2][:, :, :].rearrange("p a (k q) -> p (a k) q", q=HQ),
                                                    part, ALU.add).then_inc(k_added, 1)


def attend(nc, io, scratch, ctx_all):
    GT = 4
    VW = 32
    HALF = KT // 2
    ZSLOTS = 4
    ROW_DMAS = len(PART_A) + len(PART_B)
    with ExitStack() as ctx:
        def sb(name, shape, dt=FP32):
            return ctx.enter_context(nc.sbuf_tensor(name, shape, dt))

        def sem(name):
            return ctx.enter_context(nc.semaphore(name))

        ident = sb("a_ident", [P, P])
        q_rows = [sb(f"q_rows{i}", [ROWS, S], BF16) for i in range(2)]
        k_rows = [sb(f"k_rows{i}", [ROWS, S], BF16) for i in range(2)]
        z = [sb(f"a_z{i}", [P, S]) for i in range(ZSLOTS)]
        scores = [sb(f"scores{i}", [P, S]) for i in range(GT)]
        minus_max = sb("minus_max", [P, GT])
        probs = [sb(f"probs{i}", [P, S]) for i in range(2)]
        probs_t = [sb(f"probs_t{i}", [P, KT, GT * P]) for i in range(2)]
        v_batch = sb("v_batch", [P, 2, KT, H, DH])
        v_head = [sb(f"v_head{i}", [P, KT, VW]) for i in range(2)]
        pv_sb = sb("pv_sb", [P, P])
        inv_sum = sb("inv_sum", [P, GT])

        qk_ps = [_bank_pair(ctx, nc, f"qk_ps{i}") for i in range(2)]
        pt_ps = [ctx.enter_context(nc.psum_tensor(f"pt_ps{i}", [P, HALF, P], FP32)) for i in range(2)]
        pv_ps = ctx.enter_context(nc.psum_tensor("pv_ps", [P, 512], FP32))
        back_ps = ctx.enter_context(nc.psum_tensor("back_ps", [P, 512], FP32))

        ident_in, v_in, v_head_ready, v_head_set = sem("ident_in"), sem("v_in"), sem("v_head_ready"), sem("v_head_set")
        rows_in = [sem(f"rows_in{i}") for i in range(2)]
        z_in = [sem(f"z_in{i}") for i in range(ZSLOTS)]
        dve_passed, pool_passed = sem("a_dve_passed"), sem("a_pool_passed")
        qk_done, scores_ready, exp_done = sem("qk_done"), sem("scores_ready"), sem("exp_done")
        transposed = [sem(f"transposed{i}") for i in range(2)]
        copied = [sem(f"copied{i}") for i in range(2)]
        pv_done, pv_copied, back_done, inv_ready, ctx_written = (
            sem(n) for n in ("pv_done", "pv_copied", "back_done", "inv_ready", "ctx_written"))

        with nc.Block() as block:
            @block.sync
            def _(sp):
                def load_rows(h, slot):
                    for rows, name, pattern in ((q_rows, "q_rows", PART_A), (k_rows, "k_rows", PART_B)):
                        for g, part in enumerate(pattern):
                            sp.dma_start(rows[slot][g * DH:(g + 1) * DH, :],
                                         scratch[name][part, bass.ds(h // HG, 1), :, bass.ds(h % HG, 1), :].rearrange("g d h s -> (g d) (h s)")
                                         ).then_inc(rows_in[slot], 16)

                def load_z(h, t):
                    sp.dma_start(z[t % ZSLOTS][:, :], scratch["z"][t // HALF][bass.ds(h, 1), (t % HALF) * P:(t % HALF + 1) * P, :].rearrange(
                        "o q k -> (o q) k")).then_inc(z_in[t % ZSLOTS], 16)

                def head(h, slot, last=False):
                    if not last:
                        wait_count(sp, qk_done, h * KT)
                        load_rows(h + 1, 1 - slot)
                    for t in range(KT):
                        if not (last and t >= KT - ZSLOTS):
                            sp.wait_ge(scores_ready, h * KT + t + 1)
                            load_z(h + (t + ZSLOTS) // KT, (t + ZSLOTS) % KT)

                sp.dma_start(ident[:, :], io["ident"]).then_inc(ident_in, 16)
                load_rows(0, 0)
                for t in range(ZSLOTS):
                    load_z(0, t)
                head(0, 0)
                with sp.Fori(0, BH // 2 - 1) as i:
                    head(i * 2 + 1, 1)
                    head(i * 2 + 2, 0)
                head(BH - 1, 1, last=True)

            @block.gpsimd
            def _(pool):
                def load_v(b):
                    pool.dma_start(v_batch[:, bass.ds(b % 2, 1)].rearrange("p o t h d -> p (o t) (h d)"),
                                   scratch["v"][bass.ds(b % B, 1)].rearrange("o p t n -> (o p) t n")).then_inc(v_in, 16)

                def head_v(b, h):
                    for slot in range(2):
                        n = b * H + h
                        wait_apart(pool, pv_done, n * 2 - 1 + slot, pool_passed)
                        nc.gpsimd.tensor_copy(v_head[slot][:, :, 0:DH],
                                              v_batch[:, bass.ds(b % 2, 1), :, bass.ds(h, 1), :].rearrange("p o t i d -> p (o t i) d")
                                              ).then_inc(v_head_ready, 1)

                for slot in range(2):
                    nc.gpsimd.memset(v_head[slot][:, :, :], 0.0).then_inc(v_head_set, 1)
                pool.wait_ge(v_head_set, 2)
                for slot in range(2):
                    nc.gpsimd.memset(v_head[slot][:, :, DH:DH + 1], 1.0).then_inc(v_head_set, 1)
                pool.wait_ge(v_head_set, 4)
                load_v(0)
                pool.wait_ge(v_in, 16)
                head_v(0, 0)
                with pool.Fori(1, H) as h:
                    head_v(0, h)
                with pool.Fori(1, B) as b:
                    load_v(b)
                    wait_apart(pool, v_in, b * 16 + 16, pool_passed)
                    with pool.Fori(0, H) as h:
                        head_v(b, h)

            @block.tensor
            def _(pe):
                def scores_of(h, t, slot):
                    n = h * KT + t
                    if t == 0:
                        pe.wait_ge(rows_in[slot], (h // 2 + 1) * ROW_DMAS * 16)
                    if isinstance(n, int) and n in (2, 3):
                        pe.wait_ge(scores_ready, n - 1)
                    for c in range(S // 512):
                        ins = nc.tensor.matmul(qk_ps[t % 2][:, c, :], q_rows[slot][:, t * P:(t + 1) * P],
                                               k_rows[slot][:, c * 512:(c + 1) * 512], start=True, stop=True)
                    ins.then_inc(qk_done, 1)

                def transpose_probs(h, t, back=None):
                    n = h * KT + t
                    if isinstance(n, int) and n == 0:
                        pe.wait_ge(exp_done, 1)
                    for half in range(2):
                        wait_count(pe, copied[half], n)
                    if back is not None:
                        transpose_back(back)
                    for half in range(2):
                        for k in range(HALF):
                            kt = half * HALF + k
                            ins = nc.tensor.transpose(pt_ps[half][:, k, :], probs[t % 2][:, kt * P:(kt + 1) * P], ident[:, :])
                        ins.then_inc(transposed[half], 1)

                def products(g, slot, part):
                    if part == 0:
                        pe.wait_ge(v_head_ready, g + 1)
                    for kt in range(part * 2, part * 2 + 2):
                        for j in range(GT):
                            ins = nc.tensor.matmul(pv_ps[j * VW:(j + 1) * VW, 0:P], v_head[slot][:, kt, :],
                                                   probs_t[slot][:, kt, j * P:(j + 1) * P], start=kt == 0, stop=kt == KT - 1)
                    if part == GT - 1:
                        ins.then_inc(pv_done, 1)

                def transpose_back(g):
                    nc.tensor.transpose(back_ps[:, 0:P], pv_sb[:, :], ident[:, :]).then_inc(back_done, 1)

                def head(h, slot, first=False, last=False):
                    for t in range(KT):
                        g = h * 2 + t // GT
                        if t < KT - 2:
                            scores_of(h, t + 2, slot)
                        elif not last:
                            scores_of(h + 1, t + 2 - KT, 1 - slot)
                        if t % GT == 0 and not first:
                            products(g - 2, t // GT, GT - 1)
                        elif t % GT > 1 and not (first and t < GT):
                            products(g - 1, 1 - t // GT, t % GT - 1)
                        transpose_probs(h, t, back=g - 2 if t % GT == 2 and not first else None)
                        if t % GT == 1 and not (first and t < GT):
                            products(g - 1, 1 - t // GT, 0)

                pe.wait_ge(ident_in, 16)
                scores_of(0, 0, 0)
                scores_of(0, 1, 0)
                head(0, 0, first=True)
                with pe.Fori(0, BH // 2 - 1) as i:
                    head(i * 2 + 1, 1)
                    head(i * 2 + 2, 0)
                head(BH - 1, 1, last=True)
                groups = BH * 2
                products(groups - 2, 0, GT - 1)
                pe.wait_ge(pv_copied, groups - 1)
                pe.wait_ge(ctx_written, groups - 2)
                transpose_back(groups - 2)
                for half in range(2):
                    pe.wait_ge(copied[half], BH * KT)
                for part in range(GT):
                    products(groups - 1, 1, part)
                pe.wait_ge(pv_copied, groups)
                pe.wait_ge(ctx_written, groups - 1)
                transpose_back(groups - 1)

            @block.scalar
            def _(act):
                def exponentials(h, t):
                    n = h * KT + t
                    act.wait_ge(scores_ready, n + 1)
                    nc.scalar.activation(probs[t % 2][:, :], scores[t % GT][:, :], ACT.Exp, scale=-1.0,
                                         bias=minus_max[:, t % GT:t % GT + 1]).then_inc(exp_done, 1)

                def copy_half(h, t):
                    n, g = h * KT + t, h * 2 + t // GT
                    act.wait_ge(transposed[1], n + 1)
                    nc.scalar.activation(probs_t[t // GT][:, HALF:KT, (t % GT) * P:(t % GT + 1) * P], pt_ps[1][:, :, :],
                                         ACT.Copy).then_inc(copied[1], 1)

                def copy_products(g):
                    act.wait_ge(pv_done, g + 1)
                    nc.scalar.activation(pv_sb[:, :], pv_ps[:, 0:P], ACT.Copy).then_inc(pv_copied, 1)

                def head(h, first=False):
                    for t in range(KT):
                        exponentials(h, t)
                        if t % GT == 1 and not first:
                            copy_products(h * 2 + t // GT - 2)
                        if t > 0:
                            copy_half(h, t - 1)
                        elif not first:
                            copy_half(h - 1, KT - 1)

                head(0, first=True)
                with act.Fori(0, BH // 2 - 1) as i:
                    head(i * 2 + 1)
                    head(i * 2 + 2)
                head(BH - 1)
                groups = BH * 2
                copy_half(BH - 1, KT - 1)
                copy_products(groups - 2)
                copy_products(groups - 1)

            @block.vector
            def _(dve):
                def add_positions(h, t):
                    n = h * KT + t
                    dve.wait_ge(z_in[t % ZSLOTS], (h * 2 + t // ZSLOTS + 1) * 16)
                    wait_apart(dve, qk_done, n + 1, dve_passed)
                    nc.vector.tensor_tensor_reduce(
                        out=scores[t % GT][:, :], in0=qk_ps[t % 2][:, :, :].rearrange("p a k -> p (a k)"), in1=z[t % ZSLOTS][:, :],
                        scale=1.0, scalar=3.0e38, op0=ALU.add, op1=ALU.min,
                        accum_out=minus_max[:, t % GT:t % GT + 1]).then_inc(scores_ready, 1)

                def copy_half(h, t):
                    n, g = h * KT + t, h * 2 + t // GT
                    dve.wait_ge(transposed[0], n + 1)
                    nc.vector.tensor_copy(probs_t[t // GT][:, 0:HALF, (t % GT) * P:(t % GT + 1) * P], pt_ps[0][:, :, :]
                                          ).then_inc(copied[0], 1)

                def normalise(h, g, half):
                    dve.wait_ge(back_done, g + 1)
                    back = back_ps[:, 0:P].rearrange("q (j v) -> q j v", v=VW)
                    nc.vector.reciprocal(inv_sum[:, :], back[:, :, DH]).then_inc(inv_ready, 1)
                    dve.wait_ge(inv_ready, g + 1)
                    out = ctx_all[:, bass.ds(h, 1), half * GT:(half + 1) * GT, :].rearrange("p o j d -> p (o j) d")
                    nc.vector.tensor_tensor(out, back[:, :, 0:DH], inv_sum[:, :, None].to_broadcast([P, GT, DH]), ALU.mult
                                            ).then_inc(ctx_written, 1)

                def head(h, first=False, last=False):
                    for t in range(KT):
                        if t < KT - 1:
                            add_positions(h, t + 1)
                        elif not last:
                            add_positions(h + 1, 0)
                        if t > 0:
                            copy_half(h, t - 1)
                        elif not first:
                            copy_half(h - 1, KT - 1)
                        if t % GT == 3 and not first:
                            normalise(h - 1, h * 2 + t // GT - 2, t // GT)

                add_positions(0, 0)
                head(0, first=True)
                with dve.Fori(0, BH // 2 - 1) as i:
                    head(i * 2 + 1)
                    head(i * 2 + 2)
                head(BH - 1, last=True)
                groups = BH * 2
                copy_half(BH - 1, KT - 1)
                normalise(BH - 1, groups - 2, 0)
                normalise(BH - 1, groups - 1, 1)


def mix(nc, io, ctx_all):
    SU = SH // P
    UNITS = SU + E
    with ExitStack() as ctx:
        def sb(name, shape, dt=FP32):
            return ctx.enter_context(nc.sbuf_tensor(name, shape, dt))

        def sem(name):
            return ctx.enter_context(nc.semaphore(name))

        ident = sb("m_ident", [P, P])
        ident16 = sb("m_ident16", [P, P], BF16)
        select = sb("select", [3 * E, E, P], BF16)
        iota = sb("iota", [P, TT, E])
        minus_half = sb("m_minus_half", [P, TT])
        gate = sb("gate", [P, DC, E])
        w1 = sb("w1_sb", [P, DC, E, F])
        w2 = sb("w2_sb", [P, E, D])
        sfc1, sfc2 = (sb(n, [P, DC, SH]) for n in ("sfc1_sb", "sfc2_sb"))
        sfc3 = sb("sfc3_sb", [P, SU, D])
        x_sb = sb("m_x", [P, 2, TT, D])
        x2 = sb("x2", [P, 2, TT, D])
        xn = sb("m_xn", [P, TT, D])
        stats = sb("m_stats", [P, TT, 6])
        moments = sb("m_moments", [P, TT, 2])
        var_eps = sb("m_var_eps", [P, TT])
        rstd = sb("m_rstd", [P, TT])
        xT = [sb(f"m_xT{i}", [P, DC, TOK]) for i in range(2)]
        logits = sb("logits", [P, TT, E])
        top = sb("top", [P, TT, 8])
        top_at = sb("top_at", [P, TT, 8], U32)
        top_atf = sb("top_atf", [P, TT, 2])
        gap = sb("gap", [P, TT])
        gap_exp = sb("gap_exp", [P, TT])
        gap_exp1 = sb("gap_exp1", [P, TT])
        weight = sb("weight", [P, 2, TT])
        hit = sb("hit", [P, 2, TT, E])
        hit_w = sb("hit_w", [P, 2, TT, E])
        dispatch = sb("dispatch", [P, TT, E])
        left = sb("left", [P, 2, TT, E])
        dispatch_parts = sb("dispatch_parts", [P, TT, 3, E], BF16)
        dispatch_t = [sb(f"dispatch_t{i}", [3 * E, TOK], BF16) for i in range(2)]
        silu = [sb(f"silu{i}", [P, TOK]) for i in range(2)]
        hidden = [sb(f"hidden{i}", [P, TOK]) for i in range(2)]
        y_sb = sb("y_sb", [P, TT, D])

        psT = ctx.enter_context(nc.psum_tensor("m_psT", [P, DC, TOK], FP32))
        logits_ps = psT[:, 0, 0:TT * E].rearrange("p (t e) -> p t e", e=E)
        dispatch_ps = psT[0:3 * E, 1, 0:TOK // 2].bitcast(BF16)
        first_ps = [ctx.enter_context(nc.psum_tensor(f"first_ps{i}", [P, TOK], FP32)) for i in range(2)]
        second_ps = [ctx.enter_context(nc.psum_tensor(f"second_ps{i}", [P, TOK], FP32)) for i in range(2)]
        y_ps = ctx.enter_context(nc.psum_tensor("y_ps", [P, TT, D], FP32))

        gate_in, weights_in, consts_set = sem("gate_in"), sem("m_weights_in"), sem("m_consts_set")
        x_in = [sem("m_x_in0"), sem("m_x_in1")]
        x2_ready, stat_step, var_ready, rstd_ready, xn_ready = (
            sem(n) for n in ("x2_ready", "m_stat_step", "m_var_ready", "m_rstd_ready", "m_xn_ready"))
        xT_psum, xT_ready, logits_done, gate_step, gap_ready, gap_exp_ready = (
            sem(n) for n in ("m_xT_psum", "m_xT_ready", "logits_done", "gate_step", "gap_ready", "gap_exp_ready"))
        parts_ready, dispatch_psum, dispatch_ready = sem("parts_ready"), sem("dispatch_psum"), sem("dispatch_ready")
        unit_in, silu_ready, hidden_ready, unit_out = sem("unit_in"), sem("silu_ready"), sem("hidden_ready"), sem("unit_out")
        dve_passed, pe_passed = sem("m_dve_passed"), sem("m_pe_passed")
        y_ready, y_out = sem("y_ready"), sem("y_out")
        STAT_STEPS = 2 * TT
        GATE_STEPS = 12 + 2 * TT
        gate_loads = (("ident", ident[:, :]), ("gate_t", gate[:, :, :]), ("iota", iota[:, :, :]), ("ident16", ident16[:, :]),
                      ("select", select[:, :, :]))
        loads = (("sfc1_t", sfc1[:, :, :]), ("sfc2_t", sfc2[:, :, :]), ("sfc3_t", sfc3[:, :, :]), ("w1_t", w1[:, :, :, :]),
                 ("w2_t", w2[:, :, :]))
        ADD, STATS, AGGREGATE, NORM, TRANSPOSE, LOGITS, TOP, PLACE, GAP_EXP, WEIGHT, HIT, SPREAD, CUT, DISPATCH = (
            1, 2, 3, 4, 6, 8, 9, 10, 11, 12, 13, 14, 15, 17)

        def all_groups(engine, group):
            group(0, 0, True)
            with engine.Fori(0, GROUPS // 2 - 1) as i:
                group(i * 2 + 1, 1, True)
                group(i * 2 + 2, 0, True)
            group(GROUPS - 1, 1, False)

        def tokens_of(tensor, g):
            return tensor.rearrange("b (c t p) d -> (b c) p t d", c=S // TOK, p=P)[bass.ds(g, 1)].rearrange("o p t d -> (o p) t d")

        with nc.Block() as block:
            @block.sync
            def _(sp):
                def load_x(g, par):
                    sp.dma_start(x_sb[:, par], tokens_of(io["x"], g)).then_inc(x_in[par], 16)

                def group(g, par, more):
                    if more:
                        sp.wait_ge(x2_ready, g + 1)
                        load_x((g + 2) % GROUPS, par)
                    sp.wait_ge(y_ready, g + 1)
                    sp.dma_start(tokens_of(io["out"], g), y_sb[:, :, :]).then_inc(y_out, 16)

                for g in range(2):
                    load_x(g, g)
                for name, dst in gate_loads + loads:
                    src = io[name]
                    arrived = gate_in if (name, dst) in gate_loads else weights_in
                    if name in ("gate_t", "sfc1_t", "sfc2_t", "sfc3_t"):
                        src = src.rearrange("(c p) n -> p c n", p=P)
                    elif name == "w1_t":
                        src = src.rearrange("e (c p) f -> p c e f", p=P)
                        for c in range(DC):
                            sp.dma_start(dst[:, c], src[:, c]).then_inc(arrived, 16)
                        continue
                    elif name == "w2_t":
                        src = src.rearrange("e f d -> f e d")
                    sp.dma_start(dst, src).then_inc(arrived, 16)
                all_groups(sp, group)
                sp.wait_ge(x_in[0], (GROUPS // 2 + 1) * 16)
                sp.wait_ge(y_out, GROUPS * 16)

            @block.gpsimd
            def _(pool):
                nc.gpsimd.memset(minus_half[:, :], -0.5).then_inc(consts_set, 1)
                pool.wait_ge(consts_set, 1)
                with pool.Fori(0, GROUPS) as g:
                    pool.wait_ge(var_ready, g + 1)
                    nc.gpsimd.tensor_tensor(rstd[:, :], var_eps[:, :], minus_half[:, :], ALU.pow).then_inc(rstd_ready, 1)

            @block.vector
            def _(dve):
                steps = [0]

                def step(ins):
                    steps[0] += 1
                    ins.then_inc(gate_step, 1)

                def settle(g):
                    wait_apart(dve, gate_step, g * GATE_STEPS + steps[0], dve_passed)

                def before_units(g, par, stage):
                    if stage == ADD:
                        dve.wait_ge(x_in[par], (g // 2) * 16 + 16)
                        wait_count(dve, y_ready, g - 1)
                        for t in range(TT):
                            att = ctx_all[:, bass.ds((g // 2) * H, H), par * TT + t, :]
                            ins = nc.vector.tensor_tensor(x2[:, par, t].rearrange("p (h d) -> p h d", d=DH),
                                                          x_sb[:, par, t].rearrange("p (h d) -> p h d", d=DH), att, ALU.add)
                        ins.then_inc(x2_ready, 1)
                    elif stage == STATS:
                        dve.wait_ge(x2_ready, g + 1)
                        for t in range(TT):
                            nc.vector.bn_stats(stats[:, t], x2[:, par, t]).then_inc(stat_step, 1)
                    elif stage == AGGREGATE:
                        for t in range(TT):
                            wait_apart(dve, stat_step, g * STAT_STEPS + t + 1, dve_passed)
                            nc.vector.bn_aggr(moments[:, t], stats[:, t]).then_inc(stat_step, 1)
                        dve.wait_ge(stat_step, (g + 1) * STAT_STEPS)
                        nc.vector.tensor_scalar(var_eps[:, :], moments[:, :, 1], EPS, None, ALU.add).then_inc(var_ready, 1)
                    elif stage == NORM:
                        dve.wait_ge(rstd_ready, g + 1)
                        wait_count(dve, xT_psum, g)
                        for t in range(TT):
                            ins = nc.vector.tensor_scalar(xn[:, t], x2[:, par, t], moments[:, t, 0:1], rstd[:, t:t + 1],
                                                          ALU.subtract, ALU.mult)
                        ins.then_inc(xn_ready, 1)
                    elif stage == TOP:
                        steps[0] = 0
                        dve.wait_ge(logits_done, g + 1)
                        step(nc.vector.tensor_copy(logits[:, :, :], logits_ps))
                        settle(g)
                        for t in range(TT):
                            step(nc.vector.max(top[:, t], logits[:, t]))
                    elif stage == PLACE:
                        settle(g)
                        for t in range(TT):
                            step(nc.vector.max_index(top_at[:, t], top[:, t], logits[:, t]))
                        nc.vector.tensor_tensor(gap[:, :], top[:, :, 1], top[:, :, 0], ALU.subtract).then_inc(gap_ready, 1)
                        settle(g)
                        step(nc.vector.tensor_copy(top_atf[:, :, :], top_at[:, :, 0:2]))
                    elif stage == WEIGHT:
                        dve.wait_ge(gap_exp_ready, g + 1)
                        step(nc.vector.tensor_scalar(gap_exp1[:, :], gap_exp[:, :], 1.0, None, ALU.add))
                        settle(g)
                        step(nc.vector.reciprocal(weight[:, 0], gap_exp1[:, :]))
                        settle(g)
                        step(nc.vector.tensor_tensor(weight[:, 1], weight[:, 0], gap_exp[:, :], ALU.mult))
                    elif stage == HIT:
                        for i in range(2):
                            step(nc.vector.tensor_tensor(hit[:, i], iota[:, :, :],
                                                         top_atf[:, :, i:i + 1].to_broadcast([P, TT, E]), ALU.is_equal))
                        settle(g)
                        for i in range(2):
                            step(nc.vector.tensor_tensor(hit_w[:, i], hit[:, i],
                                                         weight[:, i, :, None].to_broadcast([P, TT, E]), ALU.mult))
                    elif stage == SPREAD:
                        settle(g)
                        step(nc.vector.tensor_tensor(dispatch[:, :, :], hit_w[:, 0], hit_w[:, 1], ALU.add))
                        settle(g)
                        wait_count(dve, dispatch_psum, g)
                        step(nc.vector.tensor_copy(dispatch_parts[:, :, 0, :], dispatch[:, :, :]))
                        settle(g)
                        step(nc.vector.tensor_tensor(left[:, 0], dispatch[:, :, :], dispatch_parts[:, :, 0, :], ALU.subtract))
                    elif stage == CUT:
                        settle(g)
                        nc.vector.tensor_copy(dispatch_parts[:, :, 1, :], left[:, 0]).then_inc(parts_ready, 1)
                        dve.wait_ge(parts_ready, g * 3 + 1)
                        nc.vector.tensor_tensor(left[:, 1], left[:, 0], dispatch_parts[:, :, 1, :], ALU.subtract).then_inc(parts_ready, 1)
                        dve.wait_ge(parts_ready, g * 3 + 2)
                        nc.vector.tensor_copy(dispatch_parts[:, :, 2, :], left[:, 1]).then_inc(parts_ready, 1)
                        assert steps[0] == GATE_STEPS, steps

                def output(g, par):
                    dve.wait_ge(unit_out, (g + 1) * UNITS)
                    wait_count(dve, y_out, g * 16)
                    nc.vector.tensor_tensor(y_sb[:, :, :], y_ps[:, :, :], x2[:, par], ALU.add).then_inc(y_ready, 1)

                def group(g, par, more):
                    for u in range(UNITS):
                        n = g * UNITS + u
                        dve.wait_ge(silu_ready, n + 1)
                        wait_count(dve, unit_out, n - 1)
                        nc.vector.tensor_tensor(hidden[u % 2][:, :], second_ps[u % 2][:, :], silu[u % 2][:, :], ALU.mult
                                                ).then_inc(hidden_ready, 1)
                        if u == 0 and not (isinstance(g, int) and g == 0):
                            output(g - 1, 1 - par)
                        if more:
                            before_units(g + 1, 1 - par, u)

                dve.wait_ge(gate_in, len(gate_loads) * 16)
                for stage in range(UNITS):
                    before_units(0, 0, stage)
                all_groups(dve, group)
                output(GROUPS - 1, 1)

            @block.tensor
            def _(pe):
                def before_units(g, par, stage):
                    if stage == TRANSPOSE:
                        pe.wait_ge(xn_ready, g + 1)
                        wait_count(pe, dispatch_ready, g)
                        for c in range(DC):
                            for t in range(TT):
                                ins = nc.tensor.transpose(psT[:, c, t * P:(t + 1) * P], xn[:, t, c * P:(c + 1) * P], ident[:, :])
                        ins.then_inc(xT_psum, 1)
                    elif stage == LOGITS:
                        pe.wait_ge(xT_ready, g + 1)
                        for t in range(TT):
                            for c in range(DC):
                                ins = nc.tensor.matmul(logits_ps[:, t, :], xT[par][:, c, t * P:(t + 1) * P], gate[:, c, :],
                                                       start=c == 0, stop=c == DC - 1)
                        ins.then_inc(logits_done, 1)
                    elif stage == DISPATCH:
                        wait_apart(pe, parts_ready, (g + 1) * 3, pe_passed)
                        for t in range(TT):
                            ins = nc.tensor.transpose(dispatch_ps[:, t * P:(t + 1) * P],
                                                      dispatch_parts[:, t].rearrange("p a e -> p (a e)"), ident16[:, :])
                        ins.then_inc(dispatch_psum, 1)

                def unit_products(g, par, u):
                    wait_count(pe, hidden_ready, g * UNITS + u - 1)
                    for c in range(DC):
                        w = sfc1[:, c, u * P:(u + 1) * P] if u < SU else w1[:, c, u - SU, :]
                        nc.tensor.matmul(first_ps[u % 2][:, :], w, xT[par][:, c, :], start=c == 0, stop=c == DC - 1)
                    if u < SU:
                        for c in range(DC):
                            ins = nc.tensor.matmul(second_ps[u % 2][:, :], sfc2[:, c, u * P:(u + 1) * P], xT[par][:, c, :],
                                                   start=c == 0, stop=c == DC - 1)
                    else:
                        if u == SU:
                            pe.wait_ge(dispatch_ready, g + 1)
                        ins = nc.tensor.matmul(second_ps[u % 2][:, :], select[:, u - SU, :], dispatch_t[par][:, :], start=True, stop=True)
                    ins.then_inc(unit_in, 1)

                def unit_output(g, u):
                    pe.wait_ge(hidden_ready, g * UNITS + u + 1)
                    if u == 0:
                        wait_count(pe, y_ready, g)
                    w = sfc3[:, u, :] if u < SU else w2[:, u - SU, :]
                    for t in range(TT):
                        ins = nc.tensor.matmul(y_ps[:, t, :], hidden[u % 2][:, t * P:(t + 1) * P], w,
                                               start=u == 0 and t % 2 == 0, stop=u == UNITS - 1, skip_group_check=True)
                    ins.then_inc(unit_out, 1)

                def group(g, par, more):
                    for u in range(UNITS):
                        unit_products(g, par, u)
                        if u > 0:
                            unit_output(g, u - 1)
                        elif not (isinstance(g, int) and g == 0):
                            unit_output(g - 1, UNITS - 1)
                        if more:
                            before_units(g + 1, 1 - par, u)

                pe.wait_ge(gate_in, len(gate_loads) * 16)
                for stage in range(UNITS):
                    before_units(0, 0, stage)
                pe.wait_ge(weights_in, (len(loads) + 1) * 16)
                all_groups(pe, group)
                unit_output(GROUPS - 1, UNITS - 1)

            @block.scalar
            def _(act):
                def before_units(g, par, stage):
                    if stage == TRANSPOSE:
                        act.wait_ge(xT_psum, g + 1)
                        nc.scalar.activation(xT[par][:, :, :], psT[:, :, :], ACT.Copy).then_inc(xT_ready, 1)
                    elif stage == GAP_EXP:
                        act.wait_ge(gap_ready, g + 1)
                        nc.scalar.activation(gap_exp[:, :], gap[:, :], ACT.Exp).then_inc(gap_exp_ready, 1)
                    elif stage == DISPATCH:
                        act.wait_ge(dispatch_psum, g + 1)
                        nc.scalar.activation(dispatch_t[par][:, :], dispatch_ps, ACT.Copy).then_inc(dispatch_ready, 1)

                def group(g, par, more):
                    for u in range(UNITS):
                        n = g * UNITS + u
                        act.wait_ge(unit_in, n + 1)
                        wait_count(act, hidden_ready, n - 1)
                        nc.scalar.activation(silu[u % 2][:, :], first_ps[u % 2][:, :], ACT.Silu).then_inc(silu_ready, 1)
                        if more:
                            before_units(g + 1, 1 - par, u)

                for stage in range(UNITS):
                    before_units(0, 0, stage)
                all_groups(act, group)


def build(nc, io, phases=("project", "position", "attend", "mix")):
    scratch = {
        "q_rows": nc.dram_tensor("q_rows_all", [3, BH // HG, DH, HG, S], BF16).ap(),
        "k_rows": nc.dram_tensor("k_rows_all", [3, BH // HG, DH, HG, S], BF16).ap(),
        "q_tiles": nc.dram_tensor("q_tiles_all", [3, S // HQ, BH // HG, DH, HG, HQ], BF16).ap(),
        "k_tiles": nc.dram_tensor("k_tiles_all", [3, S // HK, BH // HG, DH, HG, HK], BF16).ap(),
        "tables": nc.dram_tensor("tables", [2, ROWS, TABLE], BF16).ap(),
        "v": nc.dram_tensor("v_all", [B, P, KT, D], FP32).ap(),
        "z": [nc.dram_tensor(f"z_all{i}", [BH, S // 2, S], FP32).ap() for i in range(2)],
    }
    project(nc, io, scratch)
    position(nc, scratch)
    with nc.sbuf_tensor("ctx_all", [P, BH, KT, DH], FP32) as ctx_all:
        attend(nc, io, scratch, ctx_all)
        mix(nc, io, ctx_all)


def kernel(L0_attn_hidden_states, L0_attn_Wq, L0_attn_bq, L0_attn_Wk, L0_attn_bk, L0_attn_Wv, L0_attn_bv,
           L0_attn_dist_emb, L0_ffn_gate_w, L0_ffn_w1, L0_ffn_w2, L0_ffn_sfc1, L0_ffn_sfc2, L0_ffn_sfc3):
    import ml_dtypes
    import concourse.bacc as bacc
    from concourse.bass_utils import run_bass_kernel_spmd

    select = np.zeros((3, E, E, P), ml_dtypes.bfloat16)
    for e in range(E):
        select[:, e, e, :] = 1
    dist = np.asarray(L0_attn_dist_emb).T

    def width_first(a):
        a = np.asarray(a)
        return np.swapaxes(a.reshape(*a.shape[:-1], 2, HG, DH), -1, -2).reshape(a.shape)

    arrays = {
        "x": L0_attn_hidden_states, "bq": width_first(L0_attn_bq), "bk": width_first(L0_attn_bk), "bv": L0_attn_bv,
        "wq_t": width_first(np.asarray(L0_attn_Wq).T), "wk_t": width_first(np.asarray(L0_attn_Wk).T), "wv_t": np.asarray(L0_attn_Wv).T,
        "dist_t": dist, "dist_rev": dist[:, ::-1],
        "gate_t": np.asarray(L0_ffn_gate_w).T, "w1_t": np.asarray(L0_ffn_w1).transpose(0, 2, 1),
        "w2_t": np.asarray(L0_ffn_w2).transpose(0, 2, 1), "sfc1_t": np.asarray(L0_ffn_sfc1).T,
        "sfc2_t": np.asarray(L0_ffn_sfc2).T, "sfc3_t": np.asarray(L0_ffn_sfc3).T,
        "ident": np.eye(P, dtype=np.float32), "ident16": np.eye(P, dtype=ml_dtypes.bfloat16),
        "select": select.reshape(3 * E, E, P),
        "iota": np.broadcast_to(np.arange(E, dtype=np.float32), (P, TT, E)),
    }
    nc = bacc.Bacc("TRN2", target_bir_lowering=False, num_devices=1)
    io, in_map = {}, {}
    for name, a in arrays.items():
        a = np.ascontiguousarray(a)
        in_map[f"in_{name}"] = a
        io[name] = nc.dram_tensor(f"in_{name}", a.shape, mybir.dt.from_np(a.dtype), kind="ExternalInput").ap()
    io["out"] = nc.dram_tensor("out_x", [B, S, D], FP32, kind="ExternalOutput").ap()
    build(nc, io)
    return run_bass_kernel_spmd(nc, [in_map], core_ids=[0]).results[0]["out_x"]
```

```python
from contextlib import ExitStack

import numpy as np

import concourse.bass as bass
from concourse import mybir
from concourse.alu_op_type import AluOpType as ALU

FP32 = mybir.dt.float32
BF16 = mybir.dt.bfloat16
U32 = mybir.dt.uint32
ACT = mybir.ActivationFunctionType
AXIS = mybir.AxisListType

P = 128
B, S, D = 8, 1024, 256
H, DH = 16, 16
BH = B * H
HG = H // 2
E, F = 16, 128
SH = 512
MAX_POS = 512
TABLE = 2 * S
EPS = 1e-5
DC = D // P
TOK = 512
TT = TOK // P
GROUPS = B * S // TOK
KT = S // P
PART_A = (0, 0, 0, 1, 1, 2)
PART_B = (0, 1, 2, 0, 1, 0)
ROWS = len(PART_A) * DH
HQ = 64
HK = HQ
ZQ = 256
WIN = 2 * HQ + P - 1


START = 2


def wait_count(engine, semaphore, count):
    if not (isinstance(count, int) and count <= 0):
        engine.wait_ge(semaphore, count)


def wait_apart(engine, semaphore, count, passed):
    wait_count(engine, semaphore, count)
    if not isinstance(count, int):
        engine.sem_inc(passed, 1)


def all_groups(engine, group):
    group(0, 0, True)
    with engine.Fori(0, GROUPS // 2 - 1) as i:
        group(i * 2 + 1, 1, True)
        group(i * 2 + 2, 0, True)
    group(GROUPS - 1, 1, False)


def tokens_of(tensor, g):
    return tensor.rearrange("b (c t p) d -> (b c) p t d", c=S // TOK, p=P)[bass.ds(g, 1)].rearrange("o p t d -> (o p) t d")


def _bank_pair(ctx, nc, name):
    return ctx.enter_context(nc.psum_tensor(name, [P, 2, 512], FP32))


def project(nc, io, scratch):
    WIDE = 2 * DH * TABLE // P
    with ExitStack() as ctx:
        def sb(name, shape, dt=FP32):
            return ctx.enter_context(nc.sbuf_tensor(name, shape, dt))

        def sem(name):
            return ctx.enter_context(nc.semaphore(name))

        ident = sb("p_ident", [P, P])
        wq, wk, wv = (sb(n, [P, DC, D]) for n in ("wq_sb", "wk_sb", "wv_sb"))
        bias_q, bias_k, bias_k4 = (sb(n, [P, DC]) for n in ("bias_q", "bias_k", "bias_k4"))
        bias_v = sb("bias_v", [P, D])
        minus_half = sb("p_minus_half", [P, TT])
        x_sb = sb("p_x", [P, 2, TT, D])
        xn = sb("p_xn", [P, 2, TT, D])
        stats = sb("p_stats", [P, 2, TT, 6])
        moments = sb("p_moments", [P, 2, TT, 2])
        var_eps = sb("p_var_eps", [P, 2, TT])
        rstd = sb("p_rstd", [P, 2, TT])
        xT = sb("p_xT", [P, 2, DC, TOK])
        qk32 = sb("qk32", [P, 4 * TOK])
        rest = sb("rest", [P, 4 * TOK])
        parts = sb("parts", [P, 2, 3, 4, TOK], BF16)
        v_sb = sb("p_v", [P, 2, TT, D])
        table = sb("table", [DH, 2, TABLE])
        wide = sb("wide", [P, WIDE])
        wide_parts = sb("wide_parts", [P, 3, WIDE], BF16)

        psT = ctx.enter_context(nc.psum_tensor("p_psT", [P, DC, TOK], FP32))
        psQK = ctx.enter_context(nc.psum_tensor("psQK", [P, 4, TOK], FP32))
        psV = ctx.enter_context(nc.psum_tensor("psV", [P, TT, D], FP32))

        weights_in, table_in, tables_out = sem("weights_in"), sem("table_in"), sem("tables_out")
        x_in = [sem("x_in0"), sem("x_in1")]
        consts_set, table_step, part_cut, bias_set = sem("consts_set"), sem("table_step"), sem("part_cut"), sem("bias_set")
        table_filled, wide_in = sem("table_filled"), sem("wide_in")
        stat_step, var_ready, rstd_ready, xn_ready = sem("stat_step"), sem("var_ready"), sem("rstd_ready"), sem("xn_ready")
        xT_psum, xT_ready, qk_psum, v_psum = sem("xT_psum"), sem("xT_ready"), sem("qk_psum"), sem("v_psum")
        qk32_ready, part1, rest1, part2, part3 = (sem(n) for n in ("qk32_ready", "part1", "rest1", "part2", "part3"))
        v_ready = sem("v_ready")
        dve_passed = sem("p_dve_passed")
        stored = [sem("stored0"), sem("stored1")]
        STORES = 3 * 6 + 1

        with nc.Block() as block:
            @block.sync
            def _(sp):
                def load_x(g, par):
                    sp.dma_start(x_sb[:, par], tokens_of(io["x"], g)).then_inc(x_in[par], 16)

                def group(g, par, more):
                    if more:
                        sp.wait_ge(xn_ready, g + 1)
                        load_x((g + 2) % GROUPS, par)
                    for part, ready in enumerate((part1, part2, part3)):
                        sp.wait_ge(ready, g + 1)
                        for rows, first in (("q_rows", 0), ("k_rows", 2)):
                            dst = scratch[rows][part, bass.ds(g // 2 * 2, 2), :, :, par * TOK:(par + 1) * TOK]
                            sp.dma_start(dst.rearrange("g d h s -> (d h) g s"),
                                         parts[:, par, part, first:first + 2, :]).then_inc(stored[par], 16)
                        for tiles, first in (("q_tiles", 0), ("k_tiles", 2)):
                            for half in range(2):
                                dst = scratch[tiles][part, par * TOK // HK:(par + 1) * TOK // HK, bass.ds(g // 2 * 2 + half, 1)]
                                sp.dma_start(dst.rearrange("t g d h s -> (d h) (t g) s"),
                                             parts[:, par, part, first + half, :].rearrange("p (t s) -> p t s", s=HK)
                                             ).then_inc(stored[par], 16)
                    sp.wait_ge(v_ready, g + 1)
                    sp.dma_start(scratch["v"][bass.ds(g // 2, 1), :, par * TT:(par + 1) * TT, :].rearrange("o p t n -> p (o t) n"),
                                 v_sb[:, par]).then_inc(stored[par], 16)

                for par in range(2):
                    sp.sem_inc(stored[par], START)
                load_x(0, 0)
                sp.dma_start(ident[:, :], io["ident"]).then_inc(weights_in, 16)
                for w, name in ((wq, "wq_t"), (wk, "wk_t"), (wv, "wv_t")):
                    sp.dma_start(w[:, :, :], io[name].rearrange("(c p) n -> p c n", p=P)).then_inc(weights_in, 16)
                for bias, name in ((bias_q, "bq"), (bias_k, "bk")):
                    with nc.allow_non_contiguous_dma(reason="256 biases, once"):
                        sp.dma_start(bias[:, :], io[name].rearrange("(c p) -> p c", p=P)).then_inc(weights_in, 16)
                sp.dma_start(bias_v[:, :], io["bv"].rearrange("(a n) -> a n", a=1).to_broadcast([P, D])).then_inc(weights_in, 16)
                load_x(1, 1)
                low = S - MAX_POS
                n = 2 * MAX_POS - 1
                sp.dma_start(table[:, 1, 0:low], io["dist_t"][:, n - low:n]).then_inc(table_in, 16)
                sp.dma_start(table[:, 1, low:low + n], io["dist_t"]).then_inc(table_in, 16)
                sp.dma_start(table[:, 0, S - MAX_POS:S - MAX_POS + n], io["dist_rev"]).then_inc(table_in, 16)
                sp.dma_start(table[:, 0, S - MAX_POS + n:S - MAX_POS + n + low], io["dist_rev"][:, 0:low]).then_inc(table_in, 16)
                sp.wait_ge(table_filled, 3)
                for way in range(2):
                    sp.dma_start(wide[way * P // 2:(way + 1) * P // 2, :], table[:, way, :]).then_inc(wide_in, 16)
                sp.wait_ge(part_cut, 3)
                for g, part in enumerate(PART_B):
                    for way in range(2):
                        sp.dma_start(scratch["tables"][way, g * DH:(g + 1) * DH, :].rearrange("d (c j) -> (d c) j", j=WIDE),
                                     wide_parts[way * P // 2:(way + 1) * P // 2, part, :]).then_inc(tables_out, 16)
                all_groups(sp, group)
                sp.wait_ge(x_in[0], (GROUPS // 2 + 1) * 16)
                for par in range(2):
                    sp.wait_ge(stored[par], START + B * STORES * 16)
                sp.wait_ge(tables_out, 16 * 2 * len(PART_B))

            @block.gpsimd
            def _(pool):
                nc.gpsimd.memset(minus_half[:, :], -0.5).then_inc(consts_set, 1)
                pool.wait_ge(consts_set, 1)

                def group(g, par, more):
                    pool.wait_ge(var_ready, g + 1)
                    nc.gpsimd.tensor_tensor(rstd[:, par], var_eps[:, par], minus_half[:, :], ALU.pow).then_inc(rstd_ready, 1)

                all_groups(pool, group)

            @block.vector
            def _(dve):
                def normalise(g, par):
                    dve.wait_ge(x_in[par], (g // 2) * 16 + 16)
                    for t in range(TT):
                        nc.vector.bn_stats(stats[:, par, t], x_sb[:, par, t]).then_inc(stat_step, 1)
                    for t in range(TT):
                        wait_apart(dve, stat_step, g * 2 * TT + t + 1, dve_passed)
                        nc.vector.bn_aggr(moments[:, par, t], stats[:, par, t]).then_inc(stat_step, 1)
                    dve.wait_ge(stat_step, g * 2 * TT + 2 * TT)
                    nc.vector.tensor_scalar(var_eps[:, par], moments[:, par, :, 1], EPS, None, ALU.add).then_inc(var_ready, 1)
                    dve.wait_ge(rstd_ready, g + 1)
                    wait_count(dve, xT_psum, g - 1)
                    for t in range(TT):
                        ins = nc.vector.tensor_scalar(xn[:, par, t], x_sb[:, par, t], moments[:, par, t, 0:1],
                                                      rstd[:, par, t:t + 1], ALU.subtract, ALU.mult)
                    ins.then_inc(xn_ready, 1)

                def cut_tables():
                    dve.wait_ge(table_in, 64)
                    n = 2 * MAX_POS - 1
                    end = S - MAX_POS + n
                    nc.vector.tensor_copy(table[:, 1, end:TABLE], table[:, 1, end - 1:end].to_broadcast([DH, TABLE - end])
                                          ).then_inc(table_filled, 1)
                    first = S - MAX_POS
                    nc.vector.tensor_copy(table[:, 0, 0:first], table[:, 0, first:first + 1].to_broadcast([DH, first])
                                          ).then_inc(table_filled, 1)
                    nc.vector.memset(table[:, 0, TABLE - 1:TABLE], 0.0).then_inc(table_filled, 1)
                    dve.wait_ge(wide_in, 32)
                    for way, factor in ((0, -1.0), (1, 4.0)):
                        rows = wide[way * P // 2:(way + 1) * P // 2, :]
                        nc.vector.tensor_scalar(rows, rows, factor, None, ALU.mult).then_inc(table_step, 1)
                    for part in range(3):
                        dve.wait_ge(table_step, 2 + part)
                        nc.vector.tensor_copy(wide_parts[:, part], wide[:, :]).then_inc(part_cut, 1)
                        if part < 2:
                            dve.wait_ge(part_cut, part + 1)
                            nc.vector.tensor_tensor(wide[:, :], wide[:, :], wide_parts[:, part], ALU.subtract).then_inc(table_step, 1)

                def group(g, par, more):
                    if more:
                        normalise(g + 1, 1 - par)
                    dve.wait_ge(part1, g + 1)
                    wait_count(dve, part3, g)
                    nc.vector.tensor_tensor(rest[:, :], qk32[:, :], parts[:, par, 0].rearrange("p a t -> p (a t)"),
                                            ALU.subtract).then_inc(rest1, 1)
                    dve.wait_ge(v_psum, g + 1)
                    dve.wait_ge(stored[par], START + g // 2 * STORES * 16)
                    nc.vector.tensor_tensor(v_sb[:, par], psV[:, :, :], bias_v[:, None, :].to_broadcast([P, TT, D]),
                                            ALU.add).then_inc(v_ready, 1)
                    dve.wait_ge(part2, g + 1)
                    nc.vector.tensor_tensor(parts[:, par, 2].rearrange("p a t -> p (a t)"), rest[:, :],
                                            parts[:, par, 1].rearrange("p a t -> p (a t)"), ALU.subtract).then_inc(part3, 1)

                normalise(0, 0)
                dve.wait_ge(weights_in, 7 * 16)
                nc.vector.tensor_scalar(bias_k4[:, :], bias_k[:, :], -0.25, None, ALU.mult).then_inc(bias_set, 1)
                cut_tables()
                all_groups(dve, group)

            @block.tensor
            def _(pe):
                def transpose_x(g, par):
                    pe.wait_ge(xn_ready, g + 1)
                    for c in range(DC):
                        for t in range(TT):
                            ins = nc.tensor.transpose(psT[:, c, t * P:(t + 1) * P], xn[:, par, t, c * P:(c + 1) * P], ident[:, :])
                    ins.then_inc(xT_psum, 1)

                def group(g, par, more):
                    pe.wait_ge(xT_ready, g + 1)
                    wait_count(pe, qk32_ready, g * 4)
                    for slot in range(4):
                        w, half = (wq, wk)[slot // 2], slot % 2
                        for c in range(DC):
                            ins = nc.tensor.matmul(psQK[:, slot, :], w[:, c, half * P:(half + 1) * P], xT[:, par, c, :],
                                                   start=c == 0, stop=c == DC - 1)
                        ins.then_inc(qk_psum, 1)
                    if more:
                        transpose_x(g + 1, 1 - par)
                    wait_count(pe, v_ready, g)
                    for t in range(TT):
                        for c in range(DC):
                            ins = nc.tensor.matmul(psV[:, t, :], xT[:, par, c, t * P:(t + 1) * P], wv[:, c, :],
                                                   start=c == 0, stop=c == DC - 1)
                    ins.then_inc(v_psum, 1)

                pe.wait_ge(weights_in, 7 * 16)
                transpose_x(0, 0)
                all_groups(pe, group)

            @block.scalar
            def _(act):
                def copy_x(g, par):
                    act.wait_ge(xT_psum, g + 1)
                    nc.scalar.activation(xT[:, par], psT[:, :, :], ACT.Copy).then_inc(xT_ready, 1)

                def group(g, par, more):
                    wait_count(act, rest1, g)
                    for slot in range(4):
                        bias, scale = ((bias_q, 1.0), (bias_k4, -0.25))[slot // 2]
                        act.wait_ge(qk_psum, g * 4 + slot + 1)
                        nc.scalar.activation(qk32[:, slot * TOK:(slot + 1) * TOK], psQK[:, slot, :], ACT.Identity,
                                             bias=bias[:, slot % 2:slot % 2 + 1], scale=scale).then_inc(qk32_ready, 1)
                    if more:
                        copy_x(g + 1, 1 - par)
                    act.wait_ge(qk32_ready, g * 4 + 4)
                    act.wait_ge(stored[par], START + g // 2 * STORES * 16)
                    nc.scalar.activation(parts[:, par, 0].rearrange("p a t -> p (a t)"), qk32[:, :], ACT.Copy).then_inc(part1, 1)
                    act.wait_ge(rest1, g + 1)
                    nc.scalar.activation(parts[:, par, 1].rearrange("p a t -> p (a t)"), rest[:, :], ACT.Copy).then_inc(part2, 1)

                act.wait_ge(weights_in, 7 * 16)
                act.wait_ge(bias_set, 1)
                copy_x(0, 0)
                all_groups(act, group)


def position(nc, scratch):
    PER_BLOCK = 4
    QQ = S // (HQ * PER_BLOCK)
    BLOCKS = QQ * KT
    STEPS = 8
    LEAD = 4
    ORDER = [("query", 0), ("query", 1)] + [("key", step) for step in range(LEAD)]
    for step in range(2, STEPS):
        ORDER += [("query", step)] + [("key", step + LEAD - 2)] * (step + LEAD - 2 < STEPS)
    QS, KS = HQ // STEPS, P // STEPS
    PARTS = 8
    PQ = HQ // PARTS
    GROUPS6 = len(PART_A)
    with ExitStack() as ctx:
        def sb(name, shape, dt=FP32):
            return ctx.enter_context(nc.sbuf_tensor(name, shape, dt))

        def sem(name):
            return ctx.enter_context(nc.semaphore(name))

        queries = [sb(f"queries{h}", [ROWS, BH, HQ], BF16) for h in range(PER_BLOCK)]
        keys = sb("keys", [ROWS, 2, BH, HK], BF16)
        falling = [sb(f"falling{i}", [ROWS, WIN], BF16) for i in range(2)]
        rising = [sb(f"rising{i}", [ROWS, WIN], BF16) for i in range(2)]
        z = [sb(f"z{i}", [P, HQ, P]) for i in range(2)]
        q_ps = [_bank_pair(ctx, nc, f"q_ps{i}") for i in range(2)]
        k_ps = [_bank_pair(ctx, nc, f"k_ps{i}") for i in range(2)]

        keys_in = [sem(f"keys_in{half}") for half in range(2)]
        queries_in = [sem(f"queries_in{h}") for h in range(PER_BLOCK)]
        falling_in = [sem(f"falling_in{i}") for i in range(2)]
        rising_in = [sem(f"rising_in{i}") for i in range(2)]
        z_out = [[sem(f"z_out{i}_{part}") for part in range(PARTS)] for i in range(2)]
        pe_passed, sp_passed = sem("z_pe_passed"), sem("z_sp_passed")
        q_terms, q_copied, k_terms, k_added = sem("q_terms"), sem("q_copied"), sem("k_terms"), sem("k_added")

        with nc.Block() as block:
            @block.sync
            def _(sp):
                def key_tile(qq, j):
                    return j if qq % 2 == 0 else KT - 1 - j

                def load_queries(qq, h):
                    for g in range(GROUPS6):
                        sp.dma_start(queries[h][g * DH:(g + 1) * DH, :, :].rearrange("d (g h) s -> d g (h s)", h=HG),
                                     scratch["q_tiles"][PART_A[g], qq * PER_BLOCK + h].rearrange("g d h s -> d g (h s)")
                                     ).then_inc(queries_in[h], 16)

                def load_keys(kt, half):
                    for g in range(GROUPS6):
                        sp.dma_start(keys[g * DH:(g + 1) * DH, half].rearrange("d (g h) s -> d g (h s)", h=HG),
                                     scratch["k_tiles"][PART_A[g], bass.ds(kt * 2 + half, 1)].rearrange("o g d h s -> d (o g) (h s)")
                                     ).then_inc(keys_in[half], 16)

                def load_falling(qq, kt, pair):
                    start = kt * P + (S - HQ - (qq * PER_BLOCK + 2 * pair + 1) * HQ)
                    sp.dma_start(falling[pair][:, :], scratch["tables"][0, :, bass.ds(start, WIN)]).then_inc(falling_in[pair], 16)

                def load_rising(qq, kt, pair):
                    start = (S - P + (qq * PER_BLOCK + 2 * pair) * HQ) - kt * P
                    sp.dma_start(rising[pair][:, :], scratch["tables"][1, :, bass.ds(start, WIN)]).then_inc(rising_in[pair], 16)

                def block_of(qq, j, kt, nxt, last=False):
                    for h in range(PER_BLOCK):
                        m = (j + qq * KT) * PER_BLOCK + h
                        if h == PER_BLOCK - 1 and not last:
                            for half in range(2):
                                wait_apart(sp, k_terms, m * STEPS + (half + 1) * STEPS // 2, sp_passed)
                                load_keys(nxt[1], half)
                        wait_apart(sp, k_added, START + (m + 1) * STEPS, sp_passed)
                        for part in range(PARTS):
                            first = qq * PER_BLOCK * HQ + h * HQ + part * PQ
                            sp.dma_start(scratch["z"][first // ZQ][:, first % ZQ:first % ZQ + PQ, bass.ds(kt * P, P)],
                                         z[h % 2][:, part * PQ:(part + 1) * PQ, :]).then_inc(z_out[h % 2][part], 16)
                        if h % 2 == 1:
                            load_rising(*nxt, h // 2)
                        wait_apart(sp, q_terms, (m + 2) * STEPS, sp_passed)
                        if h % 2 == 0:
                            load_falling(*nxt, h // 2)
                        if last and qq < QQ - 1:
                            for used in ((0, 1), (2,), (3,), ())[h]:
                                load_queries(qq + 1, used)

                for i in range(2):
                    for part in range(PARTS):
                        sp.sem_inc(z_out[i][part], START)
                for i in range(2):
                    load_queries(0, i)
                    load_falling(0, 0, i)
                    load_rising(0, 0, i)
                for half in range(2):
                    load_keys(0, half)
                for h in range(2, PER_BLOCK):
                    load_queries(0, h)
                for qq in range(QQ):
                    with sp.Fori(0, KT - 1) as j:
                        block_of(qq, j, key_tile(qq, j), (qq, key_tile(qq, j + 1)))
                    block_of(qq, KT - 1, key_tile(qq, KT - 1), ((qq + 1) % QQ, key_tile(qq, KT - 1)), last=True)
                for i in range(2):
                    for part in range(PARTS):
                        sp.wait_ge(z_out[i][part], START + BLOCKS * PER_BLOCK // 2 * 16)
                    sp.wait_ge(falling_in[i], (BLOCKS + 1) * 16)
                    sp.wait_ge(rising_in[i], (BLOCKS + 1) * 16)

            @block.tensor
            def _(pe):
                def query_terms(m, h, step):
                    wait_count(pe, q_copied, m * STEPS + step - 1)
                    last = HQ - 1 + (1 - h % 2) * HQ
                    for i in range(QS):
                        q = step * QS + i
                        ins = nc.tensor.matmul(q_ps[step % 2][:, i // 4, (i % 4) * P:(i % 4 + 1) * P], queries[h][:, :, q],
                                               falling[h // 2][:, last - q:last - q + P], start=True, stop=True)
                    ins.then_inc(q_terms, 1)

                def key_terms(m, h, step):
                    pe.wait_ge(k_added, START + m * STEPS + step - 1)
                    last = P - 1 + h % 2 * HQ
                    for i in range(KS):
                        k = step * KS + i
                        ins = nc.tensor.matmul(k_ps[step % 2][:, i // 8, (i % 8) * HQ:(i % 8 + 1) * HQ], keys[:, k // HK, :, k % HK],
                                               rising[h // 2][:, last - k:last - k + HQ], start=True, stop=True)
                    ins.then_inc(k_terms, 1)

                pe.wait_ge(queries_in[0], GROUPS6 * 16)
                pe.wait_ge(falling_in[0], 16)
                for step in range(STEPS):
                    query_terms(0, 0, step)
                with pe.Fori(0, BLOCKS) as n:
                    for h in range(PER_BLOCK):
                        m = n * PER_BLOCK + h
                        if h % 2 == 0:
                            pe.wait_ge(rising_in[h // 2], (n + 1) * 16)
                        else:
                            pe.wait_ge(falling_in[(h + 1) % PER_BLOCK // 2], (n + 1 + (h + 1) // PER_BLOCK) * 16)
                        quarter = n // KT if h < PER_BLOCK - 1 else ((n + 1) % BLOCKS) // KT
                        pe.wait_ge(queries_in[(h + 1) % PER_BLOCK], (quarter + 1) * GROUPS6 * 16)
                        for kind, step in ORDER:
                            if kind == "query":
                                query_terms(m + 1, (h + 1) % PER_BLOCK, step)
                            else:
                                if h == 0 and step % (STEPS // 2) == 0:
                                    pe.wait_ge(keys_in[step // (STEPS // 2)], (n // KT * (KT - 1) + n % KT + 1) * GROUPS6 * 16)
                                key_terms(m, h, step)

            @block.scalar
            def _(act):
                def copy(m, h, step):
                    act.wait_ge(q_terms, m * STEPS + step + 1)
                    nc.scalar.activation(z[h % 2][:, step * QS:(step + 1) * QS, :],
                                         q_ps[step % 2][:, :, :].rearrange("p a (q k) -> p (a q) k", k=P), ACT.Copy).then_inc(q_copied, 1)

                for step in range(STEPS):
                    copy(0, 0, step)
                with act.Fori(0, BLOCKS) as n:
                    for h in range(PER_BLOCK):
                        for step in range(STEPS):
                            if step % (STEPS // PARTS) == 0:
                                act.wait_ge(z_out[(h + 1) % 2][step // (STEPS // PARTS)], START + (n * 2 + (h + 1) // 2) * 16)
                            copy(n * PER_BLOCK + h + 1, (h + 1) % PER_BLOCK, step)

            @block.vector
            def _(dve):
                dve.sem_inc(k_added, START)
                with dve.Fori(0, BLOCKS) as n:
                    for h in range(PER_BLOCK):
                        m = n * PER_BLOCK + h
                        dve.wait_ge(q_copied, (m + 1) * STEPS)
                        for step in range(STEPS):
                            dve.wait_ge(k_terms, m * STEPS + step + 1)
                            part = z[h % 2][:, :, step * KS:(step + 1) * KS].rearrange("p q k -> p k q")
                            nc.vector.tensor_tensor(part, k_ps[step % 2][:, :, :].rearrange("p a (k q) -> p (a k) q", q=HQ),
                                                    part, ALU.add).then_inc(k_added, 1)


def attend(nc, io, scratch, ctx_all):
    GT = 4
    VW = 32
    HALF = KT // 2
    ZSLOTS = 4
    ROW_DMAS = len(PART_A) + len(PART_B)
    with ExitStack() as ctx:
        def sb(name, shape, dt=FP32):
            return ctx.enter_context(nc.sbuf_tensor(name, shape, dt))

        def sem(name):
            return ctx.enter_context(nc.semaphore(name))

        ident = sb("a_ident", [P, P])
        q_rows = [sb(f"q_rows{i}", [ROWS, S], BF16) for i in range(2)]
        k_rows = [sb(f"k_rows{i}", [ROWS, S], BF16) for i in range(2)]
        z = [sb(f"a_z{i}", [P, S]) for i in range(ZSLOTS)]
        scores = [sb(f"scores{i}", [P, S]) for i in range(GT)]
        minus_max = sb("minus_max", [P, GT])
        probs = [sb(f"probs{i}", [P, S]) for i in range(2)]
        probs_t = [sb(f"probs_t{i}", [P, KT, GT * P]) for i in range(2)]
        v_batch = sb("v_batch", [P, 2, KT, H, DH])
        v_head = [sb(f"v_head{i}", [P, KT, VW]) for i in range(2)]
        pv_sb = sb("pv_sb", [P, P])
        inv_sum = sb("inv_sum", [P, GT])

        qk_ps = [_bank_pair(ctx, nc, f"qk_ps{i}") for i in range(2)]
        pt_ps = [ctx.enter_context(nc.psum_tensor(f"pt_ps{i}", [P, HALF, P], FP32)) for i in range(2)]
        pv_ps = ctx.enter_context(nc.psum_tensor("pv_ps", [P, 512], FP32))
        back_ps = ctx.enter_context(nc.psum_tensor("back_ps", [P, 512], FP32))

        ident_in, v_in, v_head_ready, v_head_set = sem("ident_in"), sem("v_in"), sem("v_head_ready"), sem("v_head_set")
        rows_in = [sem(f"rows_in{i}") for i in range(2)]
        z_in = [sem(f"z_in{i}") for i in range(ZSLOTS)]
        dve_passed, pool_passed = sem("a_dve_passed"), sem("a_pool_passed")
        qk_done, scores_ready, exp_done = sem("qk_done"), sem("scores_ready"), sem("exp_done")
        transposed = [sem(f"transposed{i}") for i in range(2)]
        copied = [sem(f"copied{i}") for i in range(2)]
        pv_done, pv_copied, back_done, inv_ready, ctx_written = (
            sem(n) for n in ("pv_done", "pv_copied", "back_done", "inv_ready", "ctx_written"))

        with nc.Block() as block:
            @block.sync
            def _(sp):
                def load_rows(h, slot, batch):
                    rows, name, pattern = ((q_rows, "q_rows", PART_A), (k_rows, "k_rows", PART_B))[batch // 2]
                    for g in range(batch % 2 * 3, batch % 2 * 3 + 3):
                        sp.dma_start(rows[slot][g * DH:(g + 1) * DH, :],
                                     scratch[name][pattern[g], bass.ds(h // HG, 1), :, bass.ds(h % HG, 1), :].rearrange("g d h s -> (g d) (h s)")
                                     ).then_inc(rows_in[slot], 16)

                def load_z(h, t):
                    sp.dma_start(z[t % ZSLOTS][:, :], scratch["z"][t * P // ZQ][bass.ds(h, 1), t * P % ZQ:t * P % ZQ + P, :].rearrange(
                        "o q k -> (o q) k")).then_inc(z_in[t % ZSLOTS], 16)

                def head(h, slot, last=False):
                    if not last:
                        wait_count(sp, qk_done, h * KT)
                    for t in range(KT):
                        if not last and t < 4:
                            load_rows(h + 1, 1 - slot, t)
                        if not (last and t >= KT - ZSLOTS):
                            sp.wait_ge(scores_ready, h * KT + t + 1)
                            load_z(h + (t + ZSLOTS) // KT, (t + ZSLOTS) % KT)

                sp.dma_start(ident[:, :], io["ident"]).then_inc(ident_in, 16)
                for t in range(ZSLOTS):
                    load_rows(0, 0, t)
                    load_z(0, t)
                head(0, 0)
                with sp.Fori(0, BH // 2 - 1) as i:
                    head(i * 2 + 1, 1)
                    head(i * 2 + 2, 0)
                head(BH - 1, 1, last=True)

            @block.gpsimd
            def _(pool):
                def load_v(b):
                    pool.dma_start(v_batch[:, bass.ds(b % 2, 1)].rearrange("p o t h d -> p (o t) (h d)"),
                                   scratch["v"][bass.ds(b % B, 1)].rearrange("o p t n -> (o p) t n")).then_inc(v_in, 16)

                def head_v(b, h):
                    for slot in range(2):
                        n = b * H + h
                        wait_apart(pool, pv_done, n * 2 - 1 + slot, pool_passed)
                        nc.gpsimd.tensor_copy(v_head[slot][:, :, 0:DH],
                                              v_batch[:, bass.ds(b % 2, 1), :, bass.ds(h, 1), :].rearrange("p o t i d -> p (o t i) d")
                                              ).then_inc(v_head_ready, 1)

                for slot in range(2):
                    nc.gpsimd.memset(v_head[slot][:, :, :], 0.0).then_inc(v_head_set, 1)
                pool.wait_ge(v_head_set, 2)
                for slot in range(2):
                    nc.gpsimd.memset(v_head[slot][:, :, DH:DH + 1], 1.0).then_inc(v_head_set, 1)
                pool.wait_ge(v_head_set, 4)
                load_v(0)
                pool.wait_ge(v_in, 16)
                head_v(0, 0)
                with pool.Fori(1, H) as h:
                    head_v(0, h)
                with pool.Fori(1, B) as b:
                    load_v(b)
                    wait_apart(pool, v_in, b * 16 + 16, pool_passed)
                    with pool.Fori(0, H) as h:
                        head_v(b, h)

            @block.tensor
            def _(pe):
                def scores_of(h, t, slot):
                    n = h * KT + t
                    if t == 0:
                        pe.wait_ge(rows_in[slot], (h // 2 + 1) * ROW_DMAS * 16)
                    if isinstance(n, int) and n in (2, 3):
                        pe.wait_ge(scores_ready, n - 1)
                    for c in range(S // 512):
                        ins = nc.tensor.matmul(qk_ps[t % 2][:, c, :], q_rows[slot][:, t * P:(t + 1) * P],
                                               k_rows[slot][:, c * 512:(c + 1) * 512], start=True, stop=True)
                    ins.then_inc(qk_done, 1)

                def transpose_probs(h, t, back=None):
                    n = h * KT + t
                    if isinstance(n, int) and n == 0:
                        pe.wait_ge(exp_done, 1)
                    for half in range(2):
                        wait_count(pe, copied[half], n)
                    if back is not None:
                        transpose_back(back)
                    for half in range(2):
                        for k in range(HALF):
                            kt = half * HALF + k
                            ins = nc.tensor.transpose(pt_ps[half][:, k, :], probs[t % 2][:, kt * P:(kt + 1) * P], ident[:, :])
                        ins.then_inc(transposed[half], 1)

                def products(g, slot, part):
                    if part == 0:
                        wait_count(pe, pv_copied, g)
                        pe.wait_ge(v_head_ready, g + 1)
                    for kt in range(part * 2, part * 2 + 2):
                        for j in range(GT):
                            ins = nc.tensor.matmul(pv_ps[j * VW:(j + 1) * VW, 0:P], v_head[slot][:, kt, :],
                                                   probs_t[slot][:, kt, j * P:(j + 1) * P], start=kt == 0, stop=kt == KT - 1)
                    if part == GT - 1:
                        ins.then_inc(pv_done, 1)

                def transpose_back(g):
                    nc.tensor.transpose(back_ps[:, 0:P], pv_sb[:, :], ident[:, :]).then_inc(back_done, 1)

                def head(h, slot, first=False, last=False):
                    for t in range(KT):
                        g = h * 2 + t // GT
                        if t < KT - 2:
                            scores_of(h, t + 2, slot)
                        elif not last:
                            scores_of(h + 1, t + 2 - KT, 1 - slot)
                        if t % GT == 0 and not first:
                            products(g - 2, t // GT, GT - 1)
                        elif t % GT > 0 and not (first and t < GT):
                            products(g - 1, 1 - t // GT, t % GT - 1)
                        transpose_probs(h, t, back=g - 2 if t % GT == 2 and not first else None)

                pe.wait_ge(ident_in, 16)
                scores_of(0, 0, 0)
                scores_of(0, 1, 0)
                head(0, 0, first=True)
                with pe.Fori(0, BH // 2 - 1) as i:
                    head(i * 2 + 1, 1)
                    head(i * 2 + 2, 0)
                head(BH - 1, 1, last=True)
                groups = BH * 2
                products(groups - 2, 0, GT - 1)
                pe.wait_ge(pv_copied, groups - 1)
                pe.wait_ge(ctx_written, groups - 2)
                transpose_back(groups - 2)
                for half in range(2):
                    pe.wait_ge(copied[half], BH * KT)
                for part in range(GT):
                    products(groups - 1, 1, part)
                pe.wait_ge(pv_copied, groups)
                pe.wait_ge(ctx_written, groups - 1)
                transpose_back(groups - 1)

            @block.scalar
            def _(act):
                def exponentials(h, t):
                    n = h * KT + t
                    act.wait_ge(scores_ready, n + 1)
                    nc.scalar.activation(probs[t % 2][:, :], scores[t % GT][:, :], ACT.Exp, scale=-1.0,
                                         bias=minus_max[:, t % GT:t % GT + 1]).then_inc(exp_done, 1)

                def copy_half(h, t):
                    n, g = h * KT + t, h * 2 + t // GT
                    act.wait_ge(transposed[1], n + 1)
                    nc.scalar.activation(probs_t[t // GT][:, HALF:KT, (t % GT) * P:(t % GT + 1) * P], pt_ps[1][:, :, :],
                                         ACT.Copy).then_inc(copied[1], 1)

                def copy_products(g):
                    act.wait_ge(pv_done, g + 1)
                    nc.scalar.activation(pv_sb[:, :], pv_ps[:, 0:P], ACT.Copy).then_inc(pv_copied, 1)

                def head(h, first=False):
                    for t in range(KT):
                        exponentials(h, t)
                        if t > 0:
                            copy_half(h, t - 1)
                        elif not first:
                            copy_half(h - 1, KT - 1)
                        if t % GT == 0 and not first:
                            copy_products(h * 2 + t // GT - 2)

                head(0, first=True)
                with act.Fori(0, BH // 2 - 1) as i:
                    head(i * 2 + 1)
                    head(i * 2 + 2)
                head(BH - 1)
                groups = BH * 2
                copy_half(BH - 1, KT - 1)
                copy_products(groups - 2)
                copy_products(groups - 1)

            @block.vector
            def _(dve):
                def add_positions(h, t):
                    n = h * KT + t
                    dve.wait_ge(z_in[t % ZSLOTS], (h * 2 + t // ZSLOTS + 1) * 16)
                    wait_apart(dve, qk_done, n + 1, dve_passed)
                    nc.vector.tensor_tensor_reduce(
                        out=scores[t % GT][:, :], in0=qk_ps[t % 2][:, :, :].rearrange("p a k -> p (a k)"), in1=z[t % ZSLOTS][:, :],
                        scale=1.0, scalar=3.0e38, op0=ALU.add, op1=ALU.min,
                        accum_out=minus_max[:, t % GT:t % GT + 1]).then_inc(scores_ready, 1)

                def copy_half(h, t):
                    n, g = h * KT + t, h * 2 + t // GT
                    dve.wait_ge(transposed[0], n + 1)
                    nc.vector.tensor_copy(probs_t[t // GT][:, 0:HALF, (t % GT) * P:(t % GT + 1) * P], pt_ps[0][:, :, :]
                                          ).then_inc(copied[0], 1)

                back = back_ps[:, 0:P].rearrange("q (j v) -> q j v", v=VW)

                def invert(g):
                    dve.wait_ge(back_done, g + 1)
                    nc.vector.reciprocal(inv_sum[:, :], back[:, :, DH]).then_inc(inv_ready, 1)

                def normalise(h, g, half):
                    dve.wait_ge(inv_ready, g + 1)
                    out = ctx_all[:, bass.ds(h, 1), half * GT:(half + 1) * GT, :].rearrange("p o j d -> p (o j) d")
                    nc.vector.tensor_tensor(out, back[:, :, 0:DH], inv_sum[:, :, None].to_broadcast([P, GT, DH]), ALU.mult
                                            ).then_inc(ctx_written, 1)

                def head(h, first=False, last=False):
                    for t in range(KT):
                        if t < KT - 1:
                            add_positions(h, t + 1)
                        elif not last:
                            add_positions(h + 1, 0)
                        if t % GT == 3 and not first:
                            invert(h * 2 + t // GT - 2)
                        if t > 0:
                            copy_half(h, t - 1)
                        elif not first:
                            copy_half(h - 1, KT - 1)
                        if t % GT == 3 and not first:
                            normalise(h - 1, h * 2 + t // GT - 2, t // GT)

                add_positions(0, 0)
                head(0, first=True)
                with dve.Fori(0, BH // 2 - 1) as i:
                    head(i * 2 + 1)
                    head(i * 2 + 2)
                head(BH - 1, last=True)
                groups = BH * 2
                copy_half(BH - 1, KT - 1)
                for half in range(2):
                    invert(groups - 2 + half)
                    normalise(BH - 1, groups - 2 + half, half)


def mix(nc, io, ctx_all):
    SU = SH // P
    UNITS = SU + E
    with ExitStack() as ctx:
        def sb(name, shape, dt=FP32):
            return ctx.enter_context(nc.sbuf_tensor(name, shape, dt))

        def sem(name):
            return ctx.enter_context(nc.semaphore(name))

        ident = sb("m_ident", [P, P])
        ident16 = sb("m_ident16", [P, P], BF16)
        select = sb("select", [3 * E, E, P], BF16)
        iota = sb("iota", [P, TT, E])
        minus_half = sb("m_minus_half", [P, TT])
        gate = sb("gate", [P, DC, E])
        w1 = sb("w1_sb", [P, DC, E, F])
        w2 = sb("w2_sb", [P, E, D])
        sfc1, sfc2 = (sb(n, [P, DC, SH]) for n in ("sfc1_sb", "sfc2_sb"))
        sfc3 = sb("sfc3_sb", [P, SU, D])
        x_sb = sb("m_x", [P, 2, TT, D])
        x2 = sb("x2", [P, 2, TT, D])
        xn = sb("m_xn", [P, TT, D])
        stats = sb("m_stats", [P, TT, 6])
        moments = sb("m_moments", [P, TT, 2])
        var_eps = sb("m_var_eps", [P, TT])
        rstd = sb("m_rstd", [P, TT])
        xT = [sb(f"m_xT{i}", [P, DC, TOK]) for i in range(2)]
        logits = sb("logits", [P, TT, E])
        top = sb("top", [P, TT, 8])
        top_at = sb("top_at", [P, TT, 8], U32)
        top_atf = sb("top_atf", [P, TT, 2])
        gap = sb("gap", [P, TT])
        gap_exp = sb("gap_exp", [P, TT])
        gap_exp1 = sb("gap_exp1", [P, TT])
        weight = sb("weight", [P, 2, TT])
        hit = sb("hit", [P, 2, TT, E])
        hit_w = sb("hit_w", [P, 2, TT, E])
        dispatch = sb("dispatch", [P, TT, E])
        left = sb("left", [P, 2, TT, E])
        dispatch_parts = sb("dispatch_parts", [P, TT, 3, E], BF16)
        dispatch_t = [sb(f"dispatch_t{i}", [3 * E, TOK], BF16) for i in range(2)]
        silu = [sb(f"silu{i}", [P, TOK]) for i in range(2)]
        hidden = [sb(f"hidden{i}", [P, TOK]) for i in range(2)]
        y_sb = sb("y_sb", [P, TT, D])

        psT = ctx.enter_context(nc.psum_tensor("m_psT", [P, DC, TOK], FP32))
        logits_ps = psT[:, 0, 0:TT * E].rearrange("p (t e) -> p t e", e=E)
        dispatch_ps = psT[0:3 * E, 1, 0:TOK // 2].bitcast(BF16)
        first_ps = [ctx.enter_context(nc.psum_tensor(f"first_ps{i}", [P, TOK], FP32)) for i in range(2)]
        second_ps = [ctx.enter_context(nc.psum_tensor(f"second_ps{i}", [P, TOK], FP32)) for i in range(2)]
        y_ps = ctx.enter_context(nc.psum_tensor("y_ps", [P, TT, D], FP32))

        gate_in, weights_in, consts_set = sem("gate_in"), sem("m_weights_in"), sem("m_consts_set")
        x_in = [sem("m_x_in0"), sem("m_x_in1")]
        x2_ready, stat_step, var_ready, rstd_ready, xn_ready = (
            sem(n) for n in ("x2_ready", "m_stat_step", "m_var_ready", "m_rstd_ready", "m_xn_ready"))
        xT_psum, xT_ready, logits_done, gate_step, gap_ready, gap_exp_ready = (
            sem(n) for n in ("m_xT_psum", "m_xT_ready", "logits_done", "gate_step", "gap_ready", "gap_exp_ready"))
        parts_ready, dispatch_psum, dispatch_ready = sem("parts_ready"), sem("dispatch_psum"), sem("dispatch_ready")
        unit_in, silu_ready, hidden_ready, unit_out = sem("unit_in"), sem("silu_ready"), sem("hidden_ready"), sem("unit_out")
        dve_passed, pe_passed = sem("m_dve_passed"), sem("m_pe_passed")
        y_ready, y_out = sem("y_ready"), sem("y_out")
        STAT_STEPS = 2 * TT
        GATE_STEPS = 12 + 2 * TT
        gate_loads = (("ident", ident[:, :]), ("gate_t", gate[:, :, :]), ("iota", iota[:, :, :]), ("ident16", ident16[:, :]),
                      ("select", select[:, :, :]))
        loads = (("sfc1_t", sfc1[:, :, :]), ("sfc2_t", sfc2[:, :, :]), ("sfc3_t", sfc3[:, :, :]), ("w1_t", w1[:, :, :, :]),
                 ("w2_t", w2[:, :, :]))
        ADD, STATS, AGGREGATE, NORM, TRANSPOSE, LOGITS, TOP, PLACE, GAP_EXP, WEIGHT, HIT, SPREAD, CUT, DISPATCH = (
            1, 2, 3, 4, 6, 8, 9, 10, 11, 12, 13, 14, 15, 17)

        with nc.Block() as block:
            @block.sync
            def _(sp):
                def load_x(g, par):
                    sp.dma_start(x_sb[:, par], tokens_of(io["x"], g)).then_inc(x_in[par], 16)

                def group(g, par, more):
                    if more:
                        sp.wait_ge(x2_ready, g + 1)
                        load_x((g + 2) % GROUPS, par)
                    sp.wait_ge(y_ready, g + 1)
                    sp.dma_start(tokens_of(io["out"], g), y_sb[:, :, :]).then_inc(y_out, 16)

                for g in range(2):
                    load_x(g, g)
                for name, dst in gate_loads + loads:
                    src = io[name]
                    arrived = gate_in if (name, dst) in gate_loads else weights_in
                    if name in ("gate_t", "sfc1_t", "sfc2_t", "sfc3_t"):
                        src = src.rearrange("(c p) n -> p c n", p=P)
                    elif name == "w1_t":
                        src = src.rearrange("e (c p) f -> p c e f", p=P)
                        for c in range(DC):
                            sp.dma_start(dst[:, c], src[:, c]).then_inc(arrived, 16)
                        continue
                    elif name == "w2_t":
                        src = src.rearrange("e f d -> f e d")
                    sp.dma_start(dst, src).then_inc(arrived, 16)
                all_groups(sp, group)
                sp.wait_ge(x_in[0], (GROUPS // 2 + 1) * 16)
                sp.wait_ge(y_out, GROUPS * 16)

            @block.gpsimd
            def _(pool):
                nc.gpsimd.memset(minus_half[:, :], -0.5).then_inc(consts_set, 1)
                pool.wait_ge(consts_set, 1)
                with pool.Fori(0, GROUPS) as g:
                    pool.wait_ge(var_ready, g + 1)
                    nc.gpsimd.tensor_tensor(rstd[:, :], var_eps[:, :], minus_half[:, :], ALU.pow).then_inc(rstd_ready, 1)

            @block.vector
            def _(dve):
                steps = [0]

                def step(ins):
                    steps[0] += 1
                    ins.then_inc(gate_step, 1)

                def settle(g):
                    wait_apart(dve, gate_step, g * GATE_STEPS + steps[0], dve_passed)

                def before_units(g, par, stage):
                    if stage == ADD:
                        dve.wait_ge(x_in[par], (g // 2) * 16 + 16)
                        wait_count(dve, y_ready, g - 1)
                        for t in range(TT):
                            att = ctx_all[:, bass.ds((g // 2) * H, H), par * TT + t, :]
                            ins = nc.vector.tensor_tensor(x2[:, par, t].rearrange("p (h d) -> p h d", d=DH),
                                                          x_sb[:, par, t].rearrange("p (h d) -> p h d", d=DH), att, ALU.add)
                        ins.then_inc(x2_ready, 1)
                    elif stage == STATS:
                        dve.wait_ge(x2_ready, g + 1)
                        for t in range(TT):
                            nc.vector.bn_stats(stats[:, t], x2[:, par, t]).then_inc(stat_step, 1)
                    elif stage == AGGREGATE:
                        for t in range(TT):
                            wait_apart(dve, stat_step, g * STAT_STEPS + t + 1, dve_passed)
                            nc.vector.bn_aggr(moments[:, t], stats[:, t]).then_inc(stat_step, 1)
                        dve.wait_ge(stat_step, (g + 1) * STAT_STEPS)
                        nc.vector.tensor_scalar(var_eps[:, :], moments[:, :, 1], EPS, None, ALU.add).then_inc(var_ready, 1)
                    elif stage == NORM:
                        dve.wait_ge(rstd_ready, g + 1)
                        wait_count(dve, xT_psum, g)
                        for t in range(TT):
                            ins = nc.vector.tensor_scalar(xn[:, t], x2[:, par, t], moments[:, t, 0:1], rstd[:, t:t + 1],
                                                          ALU.subtract, ALU.mult)
                        ins.then_inc(xn_ready, 1)
                    elif stage == TOP:
                        steps[0] = 0
                        dve.wait_ge(logits_done, g + 1)
                        step(nc.vector.tensor_copy(logits[:, :, :], logits_ps))
                        settle(g)
                        for t in range(TT):
                            step(nc.vector.max(top[:, t], logits[:, t]))
                    elif stage == PLACE:
                        settle(g)
                        for t in range(TT):
                            step(nc.vector.max_index(top_at[:, t], top[:, t], logits[:, t]))
                        nc.vector.tensor_tensor(gap[:, :], top[:, :, 1], top[:, :, 0], ALU.subtract).then_inc(gap_ready, 1)
                        settle(g)
                        step(nc.vector.tensor_copy(top_atf[:, :, :], top_at[:, :, 0:2]))
                    elif stage == WEIGHT:
                        dve.wait_ge(gap_exp_ready, g + 1)
                        step(nc.vector.tensor_scalar(gap_exp1[:, :], gap_exp[:, :], 1.0, None, ALU.add))
                        settle(g)
                        step(nc.vector.reciprocal(weight[:, 0], gap_exp1[:, :]))
                        settle(g)
                        step(nc.vector.tensor_tensor(weight[:, 1], weight[:, 0], gap_exp[:, :], ALU.mult))
                    elif stage == HIT:
                        for i in range(2):
                            step(nc.vector.tensor_tensor(hit[:, i], iota[:, :, :],
                                                         top_atf[:, :, i:i + 1].to_broadcast([P, TT, E]), ALU.is_equal))
                        settle(g)
                        for i in range(2):
                            step(nc.vector.tensor_tensor(hit_w[:, i], hit[:, i],
                                                         weight[:, i, :, None].to_broadcast([P, TT, E]), ALU.mult))
                    elif stage == SPREAD:
                        settle(g)
                        step(nc.vector.tensor_tensor(dispatch[:, :, :], hit_w[:, 0], hit_w[:, 1], ALU.add))
                        settle(g)
                        wait_count(dve, dispatch_psum, g)
                        step(nc.vector.tensor_copy(dispatch_parts[:, :, 0, :], dispatch[:, :, :]))
                        settle(g)
                        step(nc.vector.tensor_tensor(left[:, 0], dispatch[:, :, :], dispatch_parts[:, :, 0, :], ALU.subtract))
                    elif stage == CUT:
                        settle(g)
                        nc.vector.tensor_copy(dispatch_parts[:, :, 1, :], left[:, 0]).then_inc(parts_ready, 1)
                        dve.wait_ge(parts_ready, g * 3 + 1)
                        nc.vector.tensor_tensor(left[:, 1], left[:, 0], dispatch_parts[:, :, 1, :], ALU.subtract).then_inc(parts_ready, 1)
                        dve.wait_ge(parts_ready, g * 3 + 2)
                        nc.vector.tensor_copy(dispatch_parts[:, :, 2, :], left[:, 1]).then_inc(parts_ready, 1)
                        assert steps[0] == GATE_STEPS, steps

                def output(g, par):
                    dve.wait_ge(unit_out, (g + 1) * UNITS)
                    wait_count(dve, y_out, g * 16)
                    nc.vector.tensor_tensor(y_sb[:, :, :], y_ps[:, :, :], x2[:, par], ALU.add).then_inc(y_ready, 1)

                def group(g, par, more):
                    for u in range(UNITS):
                        n = g * UNITS + u
                        dve.wait_ge(silu_ready, n + 1)
                        wait_count(dve, unit_out, n - 1)
                        nc.vector.tensor_tensor(hidden[u % 2][:, :], second_ps[u % 2][:, :], silu[u % 2][:, :], ALU.mult
                                                ).then_inc(hidden_ready, 1)
                        if u == 0 and not (isinstance(g, int) and g == 0):
                            output(g - 1, 1 - par)
                        if more:
                            before_units(g + 1, 1 - par, u)

                dve.wait_ge(gate_in, len(gate_loads) * 16)
                for stage in range(UNITS):
                    before_units(0, 0, stage)
                all_groups(dve, group)
                output(GROUPS - 1, 1)

            @block.tensor
            def _(pe):
                def before_units(g, par, stage):
                    if stage == TRANSPOSE:
                        pe.wait_ge(xn_ready, g + 1)
                        wait_count(pe, dispatch_ready, g)
                        for c in range(DC):
                            for t in range(TT):
                                ins = nc.tensor.transpose(psT[:, c, t * P:(t + 1) * P], xn[:, t, c * P:(c + 1) * P], ident[:, :])
                        ins.then_inc(xT_psum, 1)
                    elif stage == LOGITS:
                        pe.wait_ge(xT_ready, g + 1)
                        for t in range(TT):
                            for c in range(DC):
                                ins = nc.tensor.matmul(logits_ps[:, t, :], xT[par][:, c, t * P:(t + 1) * P], gate[:, c, :],
                                                       start=c == 0, stop=c == DC - 1)
                        ins.then_inc(logits_done, 1)
                    elif stage == DISPATCH:
                        wait_apart(pe, parts_ready, (g + 1) * 3, pe_passed)
                        for t in range(TT):
                            ins = nc.tensor.transpose(dispatch_ps[:, t * P:(t + 1) * P],
                                                      dispatch_parts[:, t].rearrange("p a e -> p (a e)"), ident16[:, :])
                        ins.then_inc(dispatch_psum, 1)

                def unit_products(g, par, u):
                    wait_count(pe, hidden_ready, g * UNITS + u - 1)
                    for c in range(DC):
                        w = sfc1[:, c, u * P:(u + 1) * P] if u < SU else w1[:, c, u - SU, :]
                        nc.tensor.matmul(first_ps[u % 2][:, :], w, xT[par][:, c, :], start=c == 0, stop=c == DC - 1)
                    if u < SU:
                        for c in range(DC):
                            ins = nc.tensor.matmul(second_ps[u % 2][:, :], sfc2[:, c, u * P:(u + 1) * P], xT[par][:, c, :],
                                                   start=c == 0, stop=c == DC - 1)
                    else:
                        if u == SU:
                            pe.wait_ge(dispatch_ready, g + 1)
                        ins = nc.tensor.matmul(second_ps[u % 2][:, :], select[:, u - SU, :], dispatch_t[par][:, :], start=True, stop=True)
                    ins.then_inc(unit_in, 1)

                def unit_output(g, u):
                    pe.wait_ge(hidden_ready, g * UNITS + u + 1)
                    if u == 0:
                        wait_count(pe, y_ready, g)
                    w = sfc3[:, u, :] if u < SU else w2[:, u - SU, :]
                    for t in range(TT):
                        ins = nc.tensor.matmul(y_ps[:, t, :], hidden[u % 2][:, t * P:(t + 1) * P], w,
                                               start=u == 0 and t % 2 == 0, stop=u == UNITS - 1, skip_group_check=True)
                    ins.then_inc(unit_out, 1)

                def group(g, par, more):
                    for u in range(UNITS):
                        unit_products(g, par, u)
                        if u > 0:
                            unit_output(g, u - 1)
                        elif not (isinstance(g, int) and g == 0):
                            unit_output(g - 1, UNITS - 1)
                        if more:
                            before_units(g + 1, 1 - par, u)

                pe.wait_ge(gate_in, len(gate_loads) * 16)
                for stage in range(UNITS):
                    before_units(0, 0, stage)
                pe.wait_ge(weights_in, (len(loads) + 1) * 16)
                all_groups(pe, group)
                unit_output(GROUPS - 1, UNITS - 1)

            @block.scalar
            def _(act):
                def before_units(g, par, stage):
                    if stage == TRANSPOSE:
                        act.wait_ge(xT_psum, g + 1)
                        nc.scalar.activation(xT[par][:, :, :], psT[:, :, :], ACT.Copy).then_inc(xT_ready, 1)
                    elif stage == GAP_EXP:
                        act.wait_ge(gap_ready, g + 1)
                        nc.scalar.activation(gap_exp[:, :], gap[:, :], ACT.Exp).then_inc(gap_exp_ready, 1)
                    elif stage == DISPATCH:
                        act.wait_ge(dispatch_psum, g + 1)
                        nc.scalar.activation(dispatch_t[par][:, :], dispatch_ps, ACT.Copy).then_inc(dispatch_ready, 1)

                def group(g, par, more):
                    for u in range(UNITS):
                        n = g * UNITS + u
                        act.wait_ge(unit_in, n + 1)
                        wait_count(act, hidden_ready, n - 1)
                        nc.scalar.activation(silu[u % 2][:, :], first_ps[u % 2][:, :], ACT.Silu).then_inc(silu_ready, 1)
                        if more:
                            before_units(g + 1, 1 - par, u)

                for stage in range(UNITS):
                    before_units(0, 0, stage)
                all_groups(act, group)


def build(nc, io, phases=("project", "position", "attend", "mix")):
    scratch = {
        "q_rows": nc.dram_tensor("q_rows_all", [3, BH // HG, DH, HG, S], BF16).ap(),
        "k_rows": nc.dram_tensor("k_rows_all", [3, BH // HG, DH, HG, S], BF16).ap(),
        "q_tiles": nc.dram_tensor("q_tiles_all", [3, S // HQ, BH // HG, DH, HG, HQ], BF16).ap(),
        "k_tiles": nc.dram_tensor("k_tiles_all", [3, S // HK, BH // HG, DH, HG, HK], BF16).ap(),
        "tables": nc.dram_tensor("tables", [2, ROWS, TABLE], BF16).ap(),
        "v": nc.dram_tensor("v_all", [B, P, KT, D], FP32).ap(),
        "z": [nc.dram_tensor(f"z_all{i}", [BH, ZQ + 1, S], FP32).ap() for i in range(S // ZQ)],
    }
    project(nc, io, scratch)
    position(nc, scratch)
    with nc.sbuf_tensor("ctx_all", [P, BH, KT, DH], FP32) as ctx_all:
        attend(nc, io, scratch, ctx_all)
        mix(nc, io, ctx_all)


def kernel(L0_attn_hidden_states, L0_attn_Wq, L0_attn_bq, L0_attn_Wk, L0_attn_bk, L0_attn_Wv, L0_attn_bv,
           L0_attn_dist_emb, L0_ffn_gate_w, L0_ffn_w1, L0_ffn_w2, L0_ffn_sfc1, L0_ffn_sfc2, L0_ffn_sfc3):
    import ml_dtypes
    import concourse.bacc as bacc
    from concourse.bass_utils import run_bass_kernel_spmd

    select = np.zeros((3, E, E, P), ml_dtypes.bfloat16)
    for e in range(E):
        select[:, e, e, :] = 1
    dist = np.asarray(L0_attn_dist_emb).T

    def width_first(a):
        a = np.asarray(a)
        return np.swapaxes(a.reshape(*a.shape[:-1], 2, HG, DH), -1, -2).reshape(a.shape)

    arrays = {
        "x": L0_attn_hidden_states, "bq": width_first(L0_attn_bq), "bk": width_first(L0_attn_bk), "bv": L0_attn_bv,
        "wq_t": width_first(np.asarray(L0_attn_Wq).T), "wk_t": width_first(np.asarray(L0_attn_Wk).T), "wv_t": np.asarray(L0_attn_Wv).T,
        "dist_t": dist, "dist_rev": dist[:, ::-1],
        "gate_t": np.asarray(L0_ffn_gate_w).T, "w1_t": np.asarray(L0_ffn_w1).transpose(0, 2, 1),
        "w2_t": np.asarray(L0_ffn_w2).transpose(0, 2, 1), "sfc1_t": np.asarray(L0_ffn_sfc1).T,
        "sfc2_t": np.asarray(L0_ffn_sfc2).T, "sfc3_t": np.asarray(L0_ffn_sfc3).T,
        "ident": np.eye(P, dtype=np.float32), "ident16": np.eye(P, dtype=ml_dtypes.bfloat16),
        "select": select.reshape(3 * E, E, P),
        "iota": np.broadcast_to(np.arange(E, dtype=np.float32), (P, TT, E)),
    }
    nc = bacc.Bacc("TRN2", target_bir_lowering=False, num_devices=1)
    io, in_map = {}, {}
    for name, a in arrays.items():
        a = np.ascontiguousarray(a)
        in_map[f"in_{name}"] = a
        io[name] = nc.dram_tensor(f"in_{name}", a.shape, mybir.dt.from_np(a.dtype), kind="ExternalInput").ap()
    io["out"] = nc.dram_tensor("out_x", [B, S, D], FP32, kind="ExternalOutput").ap()
    build(nc, io)
    return run_bass_kernel_spmd(nc, [in_map], core_ids=[0]).results[0]["out_x"]
```
